# Optimizing a Trainium2 kernel written in Bass

```python
import numpy as np
import jax
import jax.numpy as jnp

def _softmax(x, axis=-1):
    return jax.nn.softmax(x, axis=axis)

def _gelu(x):
    return jax.nn.gelu(x, approximate=True)

def _silu(x):
    return jax.nn.silu(x)

def _sigmoid(x):
    return jax.nn.sigmoid(x)

def _layernorm(x, axis=-1, eps=1e-05):
    m = jnp.mean(x, axis=axis, keepdims=True)
    v = jnp.var(x, axis=axis, keepdims=True)
    return (x - m) / jnp.sqrt(v + eps)

def _scatter_add(tgt, idx, src, axis=0):
    return tgt.at[idx].add(src)

def _segment_sum(src, seg, n):
    return jax.ops.segment_sum(src, seg, n)
kernel_name = 'mk_gnn_preln_d1_gnn_r8_8262ed'

def setup_inputs(seed: int=0):
    np.random.seed(seed)
    _w = jnp.asarray

    def _rec_inputs():
        import jax
        import jax.numpy as jnp
        _gk = jax.random.key(seed)
        x = -0.0002117 + 1 * jax.random.normal(jax.random.fold_in(_gk, 1), (6250, 512), jnp.float32)
        src = jax.random.randint(jax.random.fold_in(_gk, 2), (100000,), 0, 6250, jnp.int32)
        dst = jax.random.randint(jax.random.fold_in(_gk, 3), (100000,), 0, 6250, jnp.int32)
        _o = jnp.argsort(dst, stable=True)
        src = src[_o]
        dst = dst[_o]
        return (x, src, dst)
    x, src, dst = _rec_inputs()

    def _L0_gnn_setup():
        import jax, jax.numpy as jnp
        import numpy as np
        N = 6250
        E = 20000
        D = 512
        H = 512
        NEG_SLOPE = 0.01

        def _cheb_norm(src, dst, n):
            deg = jax.ops.segment_sum(jnp.ones((src.shape[0],), jnp.float32), src, num_segments=n)
            dinv = jnp.where(deg > 0, jax.lax.rsqrt(jnp.maximum(deg, 1.0)), 0.0)
            return -dinv[src] * dinv[dst]

        def _cheb_conv(x, src, dst, norm, W0, W1, b):

            def prop(h):
                return jax.ops.segment_sum(h[src] * norm[:, None], dst, num_segments=x.shape[0])
            out = x @ W0
            tx1 = prop(x)
            out = out + tx1 @ W1
            return out + b

        def _layer_norm(x, gamma, beta, eps=1e-05):
            mu = jnp.mean(x, axis=-1, keepdims=True)
            var = jnp.mean(jnp.square(x - mu), axis=-1, keepdims=True)
            return (x - mu) * jax.lax.rsqrt(var + eps) * gamma + beta
        key = jax.random.key(seed)
        ks = jax.random.split(key, 8)
        s_in = 1.0 / np.sqrt(D)
        s_h = 1.0 / np.sqrt(H)
        x = jax.random.normal(ks[0], (N, D), jnp.float32)
        edge_index = jax.random.randint(ks[1], (2, E), 0, N, dtype=jnp.int64)
        return {'x': x, 'W1_0': jax.random.normal(ks[2], (D, H), jnp.float32) * s_in, 'W1_1': jax.random.normal(ks[3], (D, H), jnp.float32) * s_in, 'b1': jnp.zeros((H,), jnp.float32), 'gamma': jnp.ones((H,), jnp.float32), 'beta': jnp.zeros((H,), jnp.float32), 'W2_0': jax.random.normal(ks[4], (H, H), jnp.float32) * s_h, 'W2_1': jax.random.normal(ks[5], (H, H), jnp.float32) * s_h, 'b2': jnp.zeros((H,), jnp.float32), 'edge_index': edge_index}
    _L0_gnn_all = _L0_gnn_setup()
    _L0_gnn_in = {k: v for k, v in _L0_gnn_all.items() if k in ('W1_0', 'W1_1', 'b1', 'gamma', 'beta', 'W2_0', 'W2_1', 'b2')}
    del _L0_gnn_all
    return {'x': x, 'src': src, 'dst': dst, 'L0_gnn_W1_0': _L0_gnn_in['W1_0'], 'L0_gnn_W1_1': _L0_gnn_in['W1_1'], 'L0_gnn_b1': _L0_gnn_in['b1'], 'L0_gnn_gamma': _L0_gnn_in['gamma'], 'L0_gnn_beta': _L0_gnn_in['beta'], 'L0_gnn_W2_0': _L0_gnn_in['W2_0'], 'L0_gnn_W2_1': _L0_gnn_in['W2_1'], 'L0_gnn_b2': _L0_gnn_in['b2']}

def reference(x, src, dst, L0_gnn_W1_0, L0_gnn_W1_1, L0_gnn_b1, L0_gnn_gamma, L0_gnn_beta, L0_gnn_W2_0, L0_gnn_W2_1, L0_gnn_b2):
    import jax
    import jax.numpy as jnp

    def _L0_gnn_ref(x, W1_0, W1_1, b1, gamma, beta, W2_0, W2_1, b2, edge_index):
        import jax, jax.numpy as jnp
        import numpy as np
        N = 6250
        E = 20000
        D = 512
        H = 512
        NEG_SLOPE = 0.01

        def _cheb_norm(src, dst, n):
            deg = jax.ops.segment_sum(jnp.ones((src.shape[0],), jnp.float32), src, num_segments=n)
            dinv = jnp.where(deg > 0, jax.lax.rsqrt(jnp.maximum(deg, 1.0)), 0.0)
            return -dinv[src] * dinv[dst]

        def _cheb_conv(x, src, dst, norm, W0, W1, b):

            def prop(h):
                return jax.ops.segment_sum(h[src] * norm[:, None], dst, num_segments=x.shape[0])
            out = x @ W0
            tx1 = prop(x)
            out = out + tx1 @ W1
            return out + b

        def _layer_norm(x, gamma, beta, eps=1e-05):
            mu = jnp.mean(x, axis=-1, keepdims=True)
            var = jnp.mean(jnp.square(x - mu), axis=-1, keepdims=True)
            return (x - mu) * jax.lax.rsqrt(var + eps) * gamma + beta
        src, dst = (edge_index[0], edge_index[1])
        norm = _cheb_norm(src, dst, x.shape[0])
        h = _cheb_conv(x, src, dst, norm, W1_0, W1_1, b1)
        h = _layer_norm(h, gamma, beta)
        h = jnp.where(h >= 0, h, NEG_SLOPE * h)
        out = _cheb_conv(h, src, dst, norm, W2_0, W2_1, b2)
        return out
    edge_index = jnp.stack([src, dst])
    h = jnp.maximum(_layernorm(x, axis=-1), 0.0)
    x = x + _L0_gnn_ref(h, L0_gnn_W1_0, L0_gnn_W1_1, L0_gnn_b1, L0_gnn_gamma, L0_gnn_beta, L0_gnn_W2_0, L0_gnn_W2_1, L0_gnn_b2, edge_index)
    return x

_drawn_inputs = setup_inputs


def setup_inputs(seed=0):
    import zlib

    import numpy as np

    out = dict(_drawn_inputs(seed))
    spreads = {'L0_gnn_b1': (0.0, 0.1),
     'L0_gnn_gamma': (1.0, 0.2),
     'L0_gnn_beta': (0.0, 0.1),
     'L0_gnn_b2': (0.0, 0.1)}
    factors = {}
    for name, (base, spread) in spreads.items():
        noise = np.random.default_rng([zlib.crc32(name.encode()), seed]).standard_normal(out[name].shape)
        drawn = base * np.exp(spread * noise) if base else spread * noise
        out[name] = jnp.asarray(drawn.astype(out[name].dtype))
    for name, factor in factors.items():
        out[name] = (out[name] * factor).astype(out[name].dtype)
    return out
```

```python
from contextlib import ExitStack

import concourse.bass as bass
from concourse import mybir

F32 = mybir.dt.float32
I32 = mybir.dt.int32
U32 = mybir.dt.uint32
BF16 = mybir.dt.bfloat16
ALU = mybir.AluOpType
ACT = mybir.ActivationFunctionType
AX_X = mybir.AxisListType.X

P = 128
EPS = 1e-5
SLOPE = 0.01


class Count:

    def __init__(self, sem, base=0):
        self.sem, self.base, self.n = sem, base, 0

    def add(self, instruction):
        instruction.then_inc(self.sem, 1)
        self.n += 1

    def settle(self, engine):
        engine.wait_ge(self.sem, self.base + self.n)


def gnn_kernel(nc, x, src, dst, W10, W11, b1, gamma, beta, W20, W21, b2, out):
    N, D = x.shape
    E = src.shape[0]
    KC = D // P
    TR = 125
    NT = N // TR
    TA = 112
    IN = 32
    GJ = 5
    NG = NT // GJ
    SLOTS = 17
    CAP = SLOTS * P
    GW = 4
    EP = 125
    EC = E // EP
    HB = EC // NT
    TILE_SHIFT = 22
    TILE_MUL = -(-2**TILE_SHIFT // TR)
    assert NT * TR == N and NT == GJ * NG and EP * EC == E and HB * NT == EC and NT % 2 == 0
    for node in range(N):
        exact = node * TILE_MUL
        for near in (exact * (1 - 2.0**-23), exact * (1 + 2.0**-23)):
            assert int(near) >> TILE_SHIFT == node // TR and near < 2**31

    table = [nc.dram_tensor(f"table{n}", [N, D], F32, kind="Internal").ap() for n in range(2)]

    ctx = ExitStack()
    with ctx:
        def sb(name, shape, dt=F32):
            return ctx.enter_context(nc.sbuf_tensor(name, shape, dt))

        def sem(name):
            return ctx.enter_context(nc.semaphore(name))

        acc = sb("acc", [P, NT * D])
        rows = sb("rows", [P, SLOTS, D])
        hots = sb("hots", [P, SLOTS * P])
        wA = sb("wA", [P, KC, D])
        wB = sb("wB", [P, KC, D])
        wC = sb("wC", [P, KC, D])
        bias = sb("bias", [P, D])
        gam = sb("gam", [P, D])
        bet = sb("bet", [P, D])
        ident = sb("ident", [P, P])
        iota_f = sb("iota_f", [P, P])
        iota_b = sb("iota_b", [P, P], BF16)
        part_i = sb("part_i", [P, 1], I32)
        part_f = sb("part_f", [P, 1])
        base_i = sb("base_i", [P, NT], I32)
        base_f = sb("base_f", [P, NT])
        idx_all = sb("idx_all", [P, NT * SLOTS], I32)
        loc_all = sb("loc_all", [P, NT * SLOTS])
        idx_now = sb("idx_now", [P, 2, SLOTS], I32)
        loc_now = sb("loc_now", [P, 2, SLOTS])
        src_i = sb("src_i", [EP, EC], I32)
        dst_f = sb("dst_f", [EP, EC])
        work = sb("work", [P, 9, D])
        rstd_all = sb("rstd_all", [P, NT])
        nmr_all = sb("nmr_all", [P, NT])
        dinv = sb("dinv", [P, NT])
        ndinv = sb("ndinv", [P, NT])
        ones = sb("ones", [P, 1])
        zeros_b = sb("zeros_b", [P, P], BF16)
        stats = sb("stats", [P, GJ, 6])
        mv = sb("mv", [P, GJ, 2])
        veps = sb("veps", [P, GJ])
        std = sb("std", [P, GJ])
        nxt_i = sb("nxt_i", [EP, 1], I32)
        viol = sb("viol", [EP, 2])
        cnt_col = sb("cnt_col", [NT, 1])
        flag_f = sb("flag_f", [1, 1])
        flag_i = sb("flag_i", [1, 1], I32)
        gen_idx = sb("gen_idx", [EP, 1], I32)
        gen_loc = sb("gen_loc", [EP, 1])
        gen_hot = sb("gen_hot", [EP, P])
        r_now = sb("r_now", [EP, 2, HB])

        txs, txT, hid, hid1, hidT = (work[:, n, :] for n in range(5))
        xin = work[:, 5, :]
        stage = [work[:, 6, :], work[:, 7, :]]
        gen_rows = work[0:EP, 8, :]

        small = work[:, 0:2, :].rearrange("p a b -> p (a b)").rearrange("p (n c) -> p n c", c=64)
        scale2, bias2, deg1, sqdeg, hasdeg, dcount = (small[:, n, 0:NT] for n in range(6))
        upper = small[0:NT, 6, 0:NT]
        row_a, row_b = small[0:1, 7, 0:NT], small[0:1, 8, 0:NT]
        cnt_row = small[0:1, 9, 0:NT + 1]
        start_i = small[0:1, 10, 0:NT].bitcast(I32)
        iota_i = work[:, 8, 0:P].bitcast(I32)

        xr = rows[:, 0:GJ, :]
        hr = rows[:, GJ:2 * GJ, :]
        r_f = rows[:, 2 * GJ:2 * GJ + 2, :].rearrange("p a b -> p (a b)")[0:EP, 0:EC]
        q_b = wB[:, :, :].rearrange("p a b -> p (a b)").bitcast(BF16)[0:EP, 0:2 * EC]
        qhot = wC[:, :, :].rearrange("p a b -> p (a b)").bitcast(BF16)[0:EP, 0:2 * HB * 2 * NT]
        rhot = hots[:, :].bitcast(BF16)[0:EP, 0:2 * HB * P]
        tmp1 = work[:, 0:2, :].rearrange("p a b -> p (a b)").bitcast(I32)[0:EP, 0:EC]
        tmp2 = work[:, 2:4, :].rearrange("p a b -> p (a b)").bitcast(I32)[0:EP, 0:EC]
        dst_i = work[:, 5:7, :].rearrange("p a b -> p (a b)").bitcast(I32)[0:EP, 0:EC]
        sortcmp = work[:, 2:4, :].rearrange("p a b -> p (a b)")[0:EP, 0:EC]
        dst_all = work[:, 5:7, :].rearrange("p a b -> p (a b)").bitcast(I32)[:, 0:NT * SLOTS]
        hT = stage

        ps = [ctx.enter_context(nc.psum_tensor(f"ps{n}", [P, 512], F32)) for n in range(7)]
        dense_ps, tr_ps, hist_ps, misc_ps = [ps[0], ps[1]], [ps[2], ps[3]], ps[5], ps[6]
        tx_ps, mm_ps = [ps[0], ps[1]], ps[4]

        s_src, s_dst, s_nxt = sem("src_in"), sem("dst_in"), sem("nxt_in")
        s_wA, s_wB, s_wC, s_wD = sem("w10_in"), sem("w11_in"), sem("w20_in"), sem("w21_in")
        s_b1, s_b2, s_gb = sem("b1_in"), sem("b2_in"), sem("gamma_beta_in")
        s_iota = sem("iota_done")
        s_const = sem("constants_done")
        s_setup = sem("setup_steps")
        s_ids = sem("edge_ids_ready")
        s_x = [sem(f"x_in{j}") for j in range(GJ)]
        s_aggr = sem("stats_steps")
        s_var, s_std, s_norm = sem("var_ready"), sem("std_ready"), sem("norm_ready")
        s_h = sem("h_ready")
        s_tr = sem("hT_in_psum")
        s_hT = sem("hT_ready")
        s_dense = sem("dense_ready")
        s_acc = sem("acc_stored")
        s_rhot, s_qhot, s_hist = sem("rhot_ready"), sem("qhot_ready"), sem("hist_read")
        s_rcol = sem("r_now_copied")
        s_histend = sem("hist_ready")
        s_post = sem("post_steps")
        s_deg1, s_sqdeg = sem("deg_ready"), sem("sqrt_deg_ready")
        s_dcount, s_counts, s_cntcol, s_starts = (sem("dcount_ready"), sem("counts_in_psum"),
                                                  sem("cnt_col_ready"), sem("starts_in_psum"))
        s_startok = sem("start_index_ready")
        s_scale2 = sem("scale2_ready")
        s_flag = sem("flag_ready")
        s_idx = sem("edge_slots_in")
        s_loc = sem("loc_ready")
        s_x2 = [sem(f"x_again_in{j}") for j in range(GJ)]
        s_hs = sem("hs_ready")
        s_tab = [sem(f"table0_out{j}") for j in range(GJ)]
        s_gath = [sem(f"slot_rows_in{c}") for c in range(SLOTS)]
        s_pass, s_dpass = sem("pool_passed"), sem("vector_passed")
        s_idxc = sem("idx_copied")
        s_locc = sem("loc_copied")
        s_hot = sem("hot_ready")
        s_slot = sem("slot_summed")
        s_tx = sem("tx_in_psum")
        s_txs = sem("txs_ready")
        s_t1, s_txT = sem("txT_in_psum"), sem("txT_ready")
        s_d1 = sem("dense1_in_psum")
        s_epi = sem("epilogue_steps")
        s_evar, s_estd, s_enorm, s_en = (sem("epi_var_ready"), sem("epi_std_ready"),
                                         sem("epi_norm_ready"), sem("normalized_ready"))
        s_h1 = sem("h1_ready")
        s_t2, s_h1T = sem("h1T_in_psum"), sem("h1T_ready")
        s_d2 = sem("dense2_in_psum")
        s_acc2 = sem("acc2_stored")
        s_xb = sem("residual_plus_bias")
        s_xr = sem("residual_in")
        s_hs1 = sem("hs1_ready")
        s_tab1 = [sem(f"table1_out{u}") for u in range(2)]
        s_fin = sem("out_ready")
        s_out = [sem(f"out_out{u}") for u in range(2)]
        s_greset = sem("gen_rows_in_reset")
        s_gidx, s_ggath, s_gloc, s_ghot, s_gmm = (sem("gen_idx_copied"), sem("gen_rows_in"),
                                                  sem("gen_loc_ready"), sem("gen_hot_ready"),
                                                  sem("gen_slot_summed"))

        block = ctx.enter_context(nc.Block())

        def acc_of(t):
            return acc[:, bass.ds(t * D, D)]

        def col(a, t):
            return a[:, bass.ds(t, 1)]

        K_EPI = 6

        @block.sync
        def _(sp):
            def rows_of(array, t, n0, n1):
                return array[bass.ds(t * TR + n0, n1 - n0), :]

            def load_tile(target, array, t, s):
                for n0, n1 in ((0, TA), (TA, TR)):
                    sp.dma_start(target[n0:n1, :], rows_of(array, t, n0, n1)).then_inc(s, 16)

            def store_tile(array, t, source, s):
                for n0, n1 in ((0, TA), (TA, TR)):
                    sp.dma_start(rows_of(array, t, n0, n1), source[n0:n1, :]).then_inc(s, 16)

            sp.dma_start(src_i[:, :], src.rearrange("(p c) -> p c", p=EP)).then_inc(s_src, 16)
            sp.dma_start(dst_i, dst.rearrange("(p c) -> p c", p=EP)).then_inc(s_dst, 16)
            sp.wait_ge(s_setup, 4)
            for j in range(GJ):
                load_tile(xr[:, j, :], x, j, s_x[j])
            sp.dma_start(wA[:, :, :], W10.rearrange("(k p) n -> p k n", p=P)).then_inc(s_wA, 16)
            sp.dma_start(bias[:, :], b1.partition_broadcast(P)).then_inc(s_b1, 16)
            with nc.allow_non_contiguous_dma(reason="first edge of each row of the edge list"):
                sp.dma_start(nxt_i[0:EP - 1, :],
                             dst[EC:E].rearrange("(p c) -> p c", c=EC)[:, 0:1]).then_inc(s_nxt, 16)
            sp.dma_start(gam[:, :], gamma.partition_broadcast(P)).then_inc(s_gb, 16)
            sp.dma_start(bet[:, :], beta.partition_broadcast(P)).then_inc(s_gb, 16)

            with sp.Fori(1, NG) as g:
                for j in range(GJ):
                    t = g * GJ + j
                    sp.wait_ge(s_h, t - GJ + 1)
                    load_tile(xr[:, j, :], x, t, s_x[j])

            sp.wait_ge(s_startok, 1)
            with sp.Fori(0, NT) as i:
                first = sp.value_load(start_i[0:1, bass.ds(i, 1)], min_val=0, max_val=E - CAP)
                sp.dma_start(idx_all[:, bass.ds(i * SLOTS, SLOTS)],
                             src[bass.ds(first, CAP)].rearrange("(p c) -> p c", p=P)).then_inc(s_idx, 16)
                sp.dma_start(dst_all[:, bass.ds(i * SLOTS, SLOTS)],
                             dst[bass.ds(first, CAP)].rearrange("(p c) -> p c", p=P)).then_inc(s_idx, 16)

            sp.wait_ge(s_h, NT)
            for j in range(GJ):
                load_tile(xr[:, j, :], x, j, s_x2[j])

            def table_group(g, more):
                for j in range(GJ):
                    t = g * GJ + j
                    sp.wait_ge(s_hs, t + 1)
                    store_tile(table[0], t, hr[:, j, :], s_tab[j])
                    if more:
                        load_tile(xr[:, j, :], x, t + GJ, s_x2[j])

            with sp.Fori(0, NG - 1) as g:
                table_group(g, True)
            table_group(NG - 1, False)

            sp.wait_ge(s_histend, 1)
            sp.dma_start(wB[:, :, :], W11.rearrange("(k p) n -> p k n", p=P)).then_inc(s_wB, 16)
            sp.dma_start(wC[:, :, :], W20.rearrange("(k p) n -> p k n", p=P)).then_inc(s_wC, 16)
            sp.wait_ge(s_acc, NT + 2)
            sp.dma_start(wA[:, :, :], W21.rearrange("(k p) n -> p k n", p=P)).then_inc(s_wD, 16)
            sp.dma_start(bias[:, :], b2.partition_broadcast(P)).then_inc(s_b2, 16)

            sp.wait_ge(s_loc, 1)
            load_tile(xin, x, 0, s_xr)

            def layer1_io(i, u, load=True):
                sp.wait_ge(s_hs1, i + 1)
                store_tile(table[1], i, stage[u], s_tab1[u])
                if load:
                    sp.wait_ge(s_acc2, i + 2)
                    load_tile(xin, x, i + 1, s_xr)

            with sp.Fori(0, NT // 2 - 1) as k:
                layer1_io(2 * k, 0)
                layer1_io(2 * k + 1, 1)
            layer1_io(NT - 2, 0)
            layer1_io(NT - 1, 1, load=False)

            with sp.Fori(0, NT // 2) as k:
                for u in range(2):
                    sp.wait_ge(s_fin, 2 * k + u + 2)
                    store_tile(out, 2 * k + u, stage[u], s_out[u])
            for u in range(2):
                sp.wait_ge(s_out[u], IN * (NT // 2 + 1))

        @block.gpsimd
        def _(pool):
            nc.gpsimd.iota(iota_i[:, :], pattern=[[1, P]], base=0, channel_multiplier=0).then_inc(s_iota, 1)
            nc.gpsimd.iota(part_i[:, :], pattern=[[1, 1]], base=0, channel_multiplier=1).then_inc(s_iota, 1)
            nc.gpsimd.iota(base_i[:, :], pattern=[[TR, NT]], base=0, channel_multiplier=0).then_inc(s_iota, 1)

            bad = {}

            def gather_tile(L, i, u):
                n = L * NT + i
                pool.wait_ge(s_slot, n * SLOTS + 1)
                nc.gpsimd.tensor_copy(idx_now[:, u, :], idx_all[:, bass.ds(i * SLOTS, SLOTS)]).then_inc(s_idxc, 1)
                pool.wait_ge(s_idxc, n + 1)
                pool.sem_inc(s_pass, 1)
                for c in range(SLOTS):
                    if c % GW == 1:
                        pool.wait_ge(s_slot, n * SLOTS + min(c + GW, SLOTS))
                        pool.sem_inc(s_pass, 1)
                    nc.gpsimd.indirect_dma_start(
                        out=rows[:, c, :], out_offset=None, in_=table[L][:, :],
                        in_offset=bass.IndirectOffsetOnAxis(ap=idx_now[:, u, c:c + 1].bitcast(U32), axis=0),
                    ).then_inc(s_gath[c], 16)
                with pool.If(bad["pool"] > 0):
                    with pool.Fori(0, EC) as e:
                        m = n * EC + e
                        pool.wait_ge(s_gmm, m + 1)
                        nc.gpsimd.tensor_copy(gen_idx[:, :], src_i[:, bass.ds(e, 1)]).then_inc(s_gidx, 1)
                        pool.wait_ge(s_gidx, m + 1)
                        pool.sem_inc(s_pass, 1)
                        nc.gpsimd.indirect_dma_start(
                            out=gen_rows, out_offset=None, in_=table[L][:, :],
                            in_offset=bass.IndirectOffsetOnAxis(ap=gen_idx[:, 0:1].bitcast(U32), axis=0),
                        ).then_inc(s_ggath, 16)
                    pool.wait_ge(s_gmm, (n + 1) * EC + 1)
                    pool.sem_inc(s_pass, 1)
                    nc.gpsimd.inc_swdge_sem([s_ggath], [16 * EC], mode="sub")
                    pool.sem_inc(s_greset, 1)

            pool.wait_ge(s_flag, 1)
            bad["pool"] = pool.value_load(flag_i[0:1, 0:1], min_val=0, max_val=1)
            pool.wait_ge(s_idx, 2 * 16 * NT)
            pool.wait_ge(s_tr, NT + GJ)
            for j in range(GJ):
                pool.wait_ge(s_tab[j], IN * (NG + 1))
            for L in range(2):
                if L == 1:
                    for u in range(2):
                        pool.wait_ge(s_tab1[u], IN * (NT // 2 + 1))
                with pool.Fori(0, NT // 2) as k:
                    gather_tile(L, 2 * k, 0)
                    gather_tile(L, 2 * k + 1, 1)

        @block.scalar
        def _(act):
            with act.Fori(0, NG) as g:
                act.wait_ge(s_var, g + 1)
                nc.scalar.activation(std[:, :], veps[:, :], ACT.Sqrt).then_inc(s_std, 1)
                act.wait_ge(s_norm, g + 1)

                def make_h(j):
                    t = g * GJ + j
                    act.wait_ge(s_x[j], IN * (g + 1))
                    act.wait_ge(s_tr, t + 1)
                    nc.scalar.activation(hr[:, j, :], xr[:, j, :], ACT.Relu, bias=col(nmr_all, t),
                                         scale=col(rstd_all, t)).then_inc(s_h, 1)

                make_h(0)
                for j in range(GJ):
                    t = g * GJ + j
                    if j + 1 < GJ:
                        make_h(j + 1)
                    act.wait_ge(s_tr, t + 1 + GJ)
                    act.wait_ge(s_dense, t + 2 if j == 0 else t + 1)
                    nc.scalar.copy(hT[j % 2], tr_ps[j % 2][:, :]).then_inc(s_hT, 1)

            act.wait_ge(s_deg1, 1)
            nc.scalar.activation(sqdeg[:, :], deg1[:, :], ACT.Sqrt).then_inc(s_sqdeg, 1)

            act.wait_ge(s_scale2, 1)
            act.wait_ge(s_tr, NT + GJ)
            with act.Fori(0, NG) as g:
                for j in range(GJ):
                    t = g * GJ + j
                    act.wait_ge(s_x2[j], IN * (g + 1))
                    act.wait_ge(s_tab[j], IN * (g + 1))
                    nc.scalar.activation(hr[:, j, :], xr[:, j, :], ACT.Relu, bias=col(bias2, t),
                                         scale=col(scale2, t)).then_inc(s_hs, 1)

            def take_tx(L, i, u):
                n = L * NT + i
                act.wait_ge(s_tx, n + 1)
                act.wait_ge(s_t1, n + 1)
                nc.scalar.activation(txs, tx_ps[u][:, :], ACT.Copy, scale=col(ndinv, i)).then_inc(s_txs, 1)

            def epilogue(L, i, u, k):
                n = L * NT + i
                act.wait_ge(s_t1, n + 2)
                act.wait_ge(s_d1, n + 1)
                nc.scalar.copy(txT, tr_ps[0][:, :]).then_inc(s_txT, 1)
                if L == 0:
                    act.wait_ge(s_evar, i + 1)
                    nc.scalar.activation(std[:, 0:1], veps[:, 0:1], ACT.Sqrt).then_inc(s_estd, 1)
                    act.wait_ge(s_enorm, i + 1)
                    nc.scalar.activation(hid1, hid, ACT.Identity, bias=veps[:, 2:3],
                                         scale=veps[:, 1:2]).then_inc(s_en, 1)
                    act.wait_ge(s_h1, i + 1)
                    act.wait_ge(s_tab1[u], IN * (k + 1))
                    nc.scalar.activation(stage[u], hid1, ACT.Copy, scale=col(dinv, i)).then_inc(s_hs1, 1)
                    act.wait_ge(s_t2, i + 1)
                    act.wait_ge(s_d2, i + 1)
                    nc.scalar.copy(hidT, tr_ps[1][:, :]).then_inc(s_h1T, 1)

            for L in range(2):
                take_tx(L, 0, 0)
                with act.Fori(0, NT // 2 - 1) as k:
                    epilogue(L, 2 * k, 0, k)
                    take_tx(L, 2 * k + 1, 1)
                    epilogue(L, 2 * k + 1, 1, k)
                    take_tx(L, 2 * k + 2, 0)
                epilogue(L, NT - 2, 0, NT // 2 - 1)
                take_tx(L, NT - 1, 1)
                epilogue(L, NT - 1, 1, NT // 2 - 1)

        @block.vector
        def _(dve):
            own = Count(s_setup)
            dve.sem_inc(s_tr, GJ)
            dve.sem_inc(s_dense, 2)
            dve.sem_inc(s_hT, 2)
            dve.sem_inc(s_acc, 2)
            dve.sem_inc(s_hist, 2)
            dve.sem_inc(s_slot, SLOTS)
            dve.sem_inc(s_t1, 1)
            dve.sem_inc(s_d1, 1)
            dve.sem_inc(s_d2, 1)
            dve.sem_inc(s_acc2, 1)
            dve.sem_inc(s_fin, 1)
            dve.sem_inc(s_gmm, 1)
            dve.sem_inc(s_greset, 1)
            for j in range(GJ):
                dve.sem_inc(s_tab[j], IN)
            for u in range(2):
                dve.sem_inc(s_tab1[u], IN)
                dve.sem_inc(s_out[u], IN)
            own.add(nc.vector.memset(xr[96:P, :, :], 0.0))
            own.add(nc.vector.memset(nxt_i[:, :], N))
            own.add(nc.vector.memset(ones[:, :], 1.0))
            own.add(nc.vector.memset(zeros_b[:, :], 0.0))
            dve.wait_ge(s_iota, 3)
            own.add(nc.vector.tensor_copy(iota_f[:, :], iota_i[:, :]))
            own.add(nc.vector.tensor_copy(iota_b[:, :], iota_i[:, :]))
            own.add(nc.vector.tensor_copy(part_f[:, :], part_i[:, :]))
            own.add(nc.vector.tensor_copy(base_f[:, :], base_i[:, :]))
            own.settle(dve)
            own.add(nc.vector.tensor_scalar(ident[:, :], iota_f[:, :], part_f[:, 0:1], None, ALU.is_equal))
            own.settle(dve)
            nc.vector.tensor_copy(flag_f[:, :], ones[0:1, 0:1]).then_inc(s_const, 1)

            def tile_of(to, nodes, tmp):
                own.add(nc.vector.tensor_scalar(tmp, nodes, float(TILE_MUL), None, ALU.mult))
                own.settle(dve)
                own.add(nc.vector.tensor_single_scalar(tmp, tmp, TILE_SHIFT, ALU.logical_shift_right))
                own.settle(dve)
                own.add(nc.vector.tensor_copy(to, tmp))

            dve.wait_ge(s_src, 16)
            tile_of(q_b[:, 0:EC], src_i[:, :], tmp1)
            own.add(nc.vector.tensor_scalar(r_f, tmp1, -float(TR), None, ALU.mult))
            own.settle(dve)
            own.add(nc.vector.tensor_tensor(r_f, r_f, src_i[:, :], ALU.add))
            dve.wait_ge(s_dst, 16)
            own.add(nc.vector.tensor_copy(dst_f[:, :], dst_i))
            tile_of(q_b[:, EC:2 * EC], dst_i, tmp2)
            own.settle(dve)
            nc.vector.tensor_copy(flag_f[:, :], ones[0:1, 0:1]).then_inc(s_ids, 1)
            own.add(nc.vector.tensor_scalar(upper[:, :], iota_f[0:NT, 0:NT], part_f[0:NT, 0:1], None, ALU.is_gt))

            dve.wait_ge(s_nxt, 16)
            own.add(nc.vector.tensor_copy(viol[:, 1:2], nxt_i[:, :]))
            own.add(nc.vector.tensor_tensor(sortcmp[:, 0:EC - 1], dst_f[:, 0:EC - 1], dst_f[:, 1:EC], ALU.is_gt))
            own.settle(dve)
            own.add(nc.vector.tensor_tensor(sortcmp[:, EC - 1:EC], dst_f[:, EC - 1:EC], viol[:, 1:2], ALU.is_gt))
            own.settle(dve)
            own.add(nc.vector.reduce_max(viol[:, 0:1], sortcmp, AX_X))
            own.settle(dve)

            tile_no = iota_b[0:EP, 0:NT].unsqueeze(1).unsqueeze(1).to_broadcast([EP, HB, 2, NT])
            q3 = q_b.rearrange("p (s c) -> p s c", s=2)

            def rhots(t, u, first_in_group):
                dve.wait_ge(s_hist, t + 2 if first_in_group else t + 1)
                nc.vector.tensor_copy(r_now[:, u, :], r_f[:, bass.ds(t * HB, HB)]).then_inc(s_rcol, 1)
                dve.wait_ge(s_rcol, t + 1)
                for c in range(HB):
                    o = rhot[:, (u * HB + c) * P:(u * HB + c + 1) * P]
                    last = nc.vector.tensor_scalar(o, iota_b[0:EP, :], r_now[:, u, c:c + 1], None, ALU.is_equal)
                last.then_inc(s_rhot, 1)
                o = qhot[:, u * HB * 2 * NT:(u + 1) * HB * 2 * NT].rearrange("p (c s n) -> p c s n", s=2, n=NT)
                q = q3[:, :, bass.ds(t * HB, HB)].rearrange("p s c -> p c s").unsqueeze(3)
                nc.vector.tensor_tensor(o, q.to_broadcast([EP, HB, 2, NT]), tile_no, ALU.is_equal).then_inc(s_qhot, 1)

            def group_stats(g):
                own = Count(s_aggr, g * 3)
                for j in range(GJ):
                    dve.wait_ge(s_x[j], IN * (g + 1))
                    last = nc.vector.bn_stats(stats[:, j, :], xr[:, j, :])
                own.add(last)
                own.settle(dve)
                dve.sem_inc(s_dpass, 1)
                for j in range(GJ):
                    last = nc.vector.bn_aggr(mv[:, j, :], stats[:, j, :])
                own.add(last)
                own.settle(dve)
                nc.vector.tensor_scalar_add(veps[:, :], mv[:, :, 1], EPS).then_inc(s_var, 1)
                dve.wait_ge(s_std, g + 1)
                own.add(nc.vector.reciprocal(rstd_all[:, bass.ds(g * GJ, GJ)], std[:, :]))
                own.settle(dve)
                nc.vector.scalar_tensor_tensor(out=nmr_all[:, bass.ds(g * GJ, GJ)], in0=mv[:, :, 0], scalar=-1.0,
                                               in1=rstd_all[:, bass.ds(g * GJ, GJ)], op0=ALU.mult,
                                               op1=ALU.mult).then_inc(s_norm, 1)

            def store_acc(t, j):
                dve.wait_ge(s_dense, t + 3)
                nc.vector.tensor_tensor(acc_of(t), dense_ps[j % 2][:, :], bias[:, :], ALU.add).then_inc(s_acc, 1)

            dve.wait_ge(s_b1, 16)
            with dve.Fori(0, NG) as g:
                group_stats(g)
                for j in range(GJ):
                    rhots(g * GJ + j, j % 2, j == 0)
                    if j:
                        store_acc(g * GJ + j - 1, j - 1)
                store_acc(g * GJ + GJ - 1, GJ - 1)

            post = Count(s_post)
            dve.wait_ge(s_histend, 1)
            nc.vector.tensor_copy(dcount[:, :], hist_ps[:, NT:2 * NT]).then_inc(s_dcount, 1)
            nc.vector.tensor_scalar_max(deg1[:, :], hist_ps[:, 0:NT], 1.0).then_inc(s_deg1, 1)
            dve.wait_ge(s_counts, 1)
            post.add(nc.vector.tensor_copy(cnt_row[:, 0:NT], misc_ps[0:1, 64:64 + NT]))
            post.add(nc.vector.tensor_copy(cnt_row[:, NT:NT + 1], misc_ps[0:1, 128:129]))
            nc.vector.tensor_copy(cnt_col[:, :], misc_ps[0:NT, 0:1]).then_inc(s_cntcol, 1)
            dve.wait_ge(s_starts, 1)
            post.add(nc.vector.tensor_scalar_min(row_a[:, :], misc_ps[0:1, 192:192 + NT], float(E - CAP)))
            post.settle(dve)
            nc.vector.tensor_copy(start_i[:, :], row_a[:, :]).then_inc(s_startok, 1)
            post.add(nc.vector.tensor_tensor(row_b[:, :], misc_ps[0:1, 192:192 + NT], row_a[:, :], ALU.subtract))
            post.settle(dve)
            post.add(nc.vector.tensor_tensor(row_b[:, :], row_b[:, :], cnt_row[:, 0:NT], ALU.add))
            post.settle(dve)
            post.add(nc.vector.tensor_scalar(row_b[:, :], row_b[:, :], float(CAP), None, ALU.is_gt))
            post.settle(dve)
            post.add(nc.vector.reduce_max(flag_f[:, :], row_b[:, :], AX_X))
            post.settle(dve)
            post.add(nc.vector.tensor_tensor(flag_f[:, :], flag_f[:, :], cnt_row[:, NT:NT + 1], ALU.max))
            post.settle(dve)
            post.add(nc.vector.tensor_scalar(flag_f[:, :], flag_f[:, :], 0.0, None, ALU.is_gt))
            post.settle(dve)
            nc.vector.tensor_copy(flag_i[:, :], flag_f[:, :]).then_inc(s_flag, 1)
            dve.wait_ge(s_sqdeg, 1)
            post.add(nc.vector.reciprocal(dinv[:, :], sqdeg[:, :]))
            post.settle(dve)
            post.add(nc.vector.tensor_scalar(hasdeg[:, :], hist_ps[:, 0:NT], 0.0, None, ALU.is_gt))
            post.settle(dve)
            post.add(nc.vector.tensor_tensor(dinv[:, :], dinv[:, :], hasdeg[:, :], ALU.mult))
            post.settle(dve)
            post.add(nc.vector.tensor_scalar_mul(ndinv[:, :], dinv[:, :], -1.0))
            post.add(nc.vector.tensor_tensor(scale2[:, :], rstd_all[:, :], dinv[:, :], ALU.mult))
            nc.vector.tensor_tensor(bias2[:, :], nmr_all[:, :], dinv[:, :], ALU.mult).then_inc(s_scale2, 1)

            dve.wait_ge(s_idx, 2 * 16 * NT)
            post.add(nc.vector.tensor_copy(loc_all[:, :], dst_all))
            post.settle(dve)
            loc3 = loc_all[:, :].rearrange("p (i c) -> p i c", c=SLOTS)
            nc.vector.tensor_tensor(loc3, loc3, base_f[:, :].unsqueeze(2).to_broadcast([P, NT, SLOTS]),
                                    ALU.subtract).then_inc(s_loc, 1)
            dve.wait_ge(s_loc, 1)
            dve.wait_ge(s_flag, 1)
            bad = dve.value_load(flag_i[0:1, 0:1], min_val=0, max_val=1)

            def copy_loc(L, i, u):
                nc.vector.tensor_copy(loc_now[:, u, :], loc_all[:, bass.ds(i * SLOTS, SLOTS)]).then_inc(s_locc, 1)
                dve.wait_ge(s_locc, L * NT + i + 1)

            def hots_of(L, i, u, slots):
                n = L * NT + i
                for c in slots:
                    dve.wait_ge(s_slot, n * SLOTS + c + 1)
                    nc.vector.tensor_scalar(hots[:, c * P:(c + 1) * P], iota_f[:, :], loc_now[:, u, c:c + 1],
                                            None, ALU.is_equal).then_inc(s_hot, 1)

            def general(L, i):
                n = L * NT + i
                with dve.If(bad > 0):
                    with dve.Fori(0, EC) as e:
                        m = n * EC + e
                        dve.wait_ge(s_gmm, m + 1)
                        nc.vector.tensor_tensor(gen_loc[:, :], dst_f[:, bass.ds(e, 1)],
                                                base_f[0:EP, bass.ds(i, 1)], ALU.subtract).then_inc(s_gloc, 1)
                        dve.wait_ge(s_gloc, m + 1)
                        nc.vector.tensor_scalar(gen_hot[:, :], iota_f[0:EP, :], gen_loc[:, 0:1], None,
                                                ALU.is_equal).then_inc(s_ghot, 1)

            def norm1(i):
                own = Count(s_epi, i * K_EPI)
                dve.wait_ge(s_d1, i + 2)
                own.add(nc.vector.tensor_tensor(hid, mm_ps[:, :], acc_of(i), ALU.add))
                own.settle(dve)
                own.add(nc.vector.bn_stats(stats[:, 0, :], hid))
                own.settle(dve)
                dve.sem_inc(s_dpass, 1)
                own.add(nc.vector.bn_aggr(mv[:, 0, :], stats[:, 0, :]))
                own.settle(dve)
                nc.vector.tensor_scalar_add(veps[:, 0:1], mv[:, 0, 1:2], EPS).then_inc(s_evar, 1)
                dve.wait_ge(s_estd, i + 1)
                own.add(nc.vector.reciprocal(veps[:, 1:2], std[:, 0:1]))
                own.settle(dve)
                nc.vector.scalar_tensor_tensor(out=veps[:, 2:3], in0=mv[:, 0, 0:1], scalar=-1.0,
                                               in1=veps[:, 1:2], op0=ALU.mult, op1=ALU.mult).then_inc(s_enorm, 1)
                dve.wait_ge(s_en, i + 1)
                own.add(nc.vector.tensor_tensor(hid, hid1, gam[:, :], ALU.mult))
                own.settle(dve)
                own.add(nc.vector.tensor_tensor(hid, hid, bet[:, :], ALU.add))
                own.settle(dve)
                nc.vector.scalar_tensor_tensor(out=hid1, in0=hid, scalar=SLOPE, in1=hid, op0=ALU.mult,
                                               op1=ALU.max).then_inc(s_h1, 1)
                assert own.n == K_EPI

            def residual1(i):
                dve.wait_ge(s_xr, IN * (i + 1))
                nc.vector.tensor_tensor(xin, xin, bias[:, :], ALU.add).then_inc(s_xb, 1)
                dve.wait_ge(s_xb, i + 1)
                dve.wait_ge(s_d2, i + 2)
                nc.vector.tensor_tensor(acc_of(i), mm_ps[:, :], xin, ALU.add).then_inc(s_acc2, 1)

            def finish2(i, u, k):
                dve.wait_ge(s_d1, NT + i + 2)
                dve.wait_ge(s_out[u], IN * (k + 1))
                nc.vector.tensor_tensor(stage[u], mm_ps[:, :], acc_of(i), ALU.add).then_inc(s_fin, 1)

            dve.wait_ge(s_gb, 32)
            dve.wait_ge(s_b2, 16)
            for L in range(2):
                def step(i, u, k_before):
                    copy_loc(L, i, u)
                    hots_of(L, i, u, range(0, 9))
                    if L == 0:
                        norm1(i - 1)
                        hots_of(L, i, u, range(9, SLOTS))
                        general(L, i)
                        residual1(i - 1)
                    else:
                        finish2(i - 1, 1 - u, k_before)
                        hots_of(L, i, u, range(9, SLOTS))
                        general(L, i)

                if L == 1:
                    for u in range(2):
                        dve.wait_ge(s_tab1[u], IN * (NT // 2 + 1))
                copy_loc(L, 0, 0)
                hots_of(L, 0, 0, range(SLOTS))
                general(L, 0)
                with dve.Fori(0, NT // 2 - 1) as k:
                    step(2 * k + 1, 1, k)
                    step(2 * k + 2, 0, k)
                step(NT - 1, 1, NT // 2 - 1)
                if L == 0:
                    norm1(NT - 1)
                    residual1(NT - 1)
                else:
                    finish2(NT - 1, 1, NT // 2 - 1)

        @block.tensor
        def _(pe):
            def transposes(to, source, signal):
                for k in range(KC):
                    last = nc.tensor.transpose(to[:, k * P:(k + 1) * P], source[:, k * P:(k + 1) * P], ident[:, :])
                for s in signal:
                    last.then_inc(s, 1)

            def dense(to, source, w, signal):
                for k in range(KC):
                    last = nc.tensor.matmul(to[:, :], source[:, k * P:(k + 1) * P], w[:, k, :],
                                            start=k == 0, stop=k == KC - 1)
                last.then_inc(signal, 1)

            def histogram(t, u):
                pe.wait_ge(s_rhot, t + 1)
                pe.wait_ge(s_qhot, t + 1)
                for c in range(HB):
                    last = nc.tensor.matmul(hist_ps[:, 0:2 * NT], rhot[:, (u * HB + c) * P:(u * HB + c + 1) * P],
                                            qhot[:, (u * HB + c) * 2 * NT:(u * HB + c + 1) * 2 * NT],
                                            start=False, stop=False)
                last.then_inc(s_hist, 1)

            def transpose_h(g, j):
                t = g * GJ + j
                pe.wait_ge(s_h, t + 1)
                pe.wait_ge(s_hT, t + 2 if j == 0 else t + 1)
                for k in range(KC):
                    last = nc.tensor.transpose(tr_ps[j % 2][:, k * P:(k + 1) * P],
                                               hr[:, j, k * P:(k + 1) * P], ident[:, :])
                last.then_inc(s_tr, 1)

            pe.wait_ge(s_const, 1)
            nc.tensor.matmul(hist_ps[:, 0:2 * NT], zeros_b[:, 0:P], zeros_b[:, 0:2 * NT], start=True, stop=False)
            pe.wait_ge(s_wA, 16)
            with pe.Fori(0, NG) as g:
                transpose_h(g, 0)
                for j in range(GJ):
                    t = g * GJ + j
                    if j + 1 < GJ:
                        transpose_h(g, j + 1)
                    histogram(t, j % 2)
                    pe.wait_ge(s_hT, t + 3)
                    pe.wait_ge(s_acc, t + 2 if j == 0 else t + 1)
                    dense(dense_ps[j % 2], hT[j % 2], wA, s_dense)
            nc.tensor.matmul(hist_ps[:, 0:2 * NT], zeros_b[:, 0:P], zeros_b[:, 0:2 * NT], start=False,
                             stop=True).then_inc(s_histend, 1)

            pe.wait_ge(s_dcount, 1)
            nc.tensor.matmul(misc_ps[0:NT, 0:1], dcount[:, :], ones[:, 0:1], start=True, stop=True)
            nc.tensor.matmul(misc_ps[0:1, 64:64 + NT], ones[:, 0:1], dcount[:, :], start=True, stop=True)
            nc.tensor.matmul(misc_ps[0:1, 128:129], viol[:, 0:1], ones[0:EP, 0:1], start=True,
                             stop=True).then_inc(s_counts, 1)
            pe.wait_ge(s_cntcol, 1)
            nc.tensor.matmul(misc_ps[0:1, 192:192 + NT], cnt_col[:, :], upper[:, :], start=True,
                             stop=True).then_inc(s_starts, 1)

            pe.wait_ge(s_flag, 1)
            bad = pe.value_load(flag_i[0:1, 0:1], min_val=0, max_val=1)

            def slots(L, i, u, which):
                n = L * NT + i
                for c in which:
                    pe.wait_ge(s_gath[c], 16 * (n + 1))
                    pe.wait_ge(s_hot, n * SLOTS + c + 1)
                    nc.tensor.matmul(tx_ps[u][:, :], hots[:, c * P:(c + 1) * P], rows[:, c, :],
                                     start=c == 0, stop=c == SLOTS - 1).then_inc(s_slot, 1)

            zero_row = zeros_b[:, 0:1].to_broadcast([P, D])

            def close(L, i, u):
                n = L * NT + i
                with pe.If(bad > 0):
                    pe.wait_ge(s_greset, n + 1)
                    nc.tensor.matmul(tx_ps[u][:, :], zeros_b[:, :], zero_row, start=True, stop=False)
                    with pe.Fori(0, EC) as e:
                        m = n * EC + e
                        pe.wait_ge(s_ggath, 16 * (e + 1))
                        pe.wait_ge(s_ghot, m + 1)
                        nc.tensor.matmul(tx_ps[u][:, :], gen_hot[:, :], gen_rows, start=False,
                                         stop=False).then_inc(s_gmm, 1)
                    nc.tensor.matmul(tx_ps[u][:, :], zeros_b[:, :], zero_row, start=False, stop=True)
                nc.tensor.matmul(tx_ps[u][:, 0:P], zeros_b[:, 0:P], zeros_b[:, 0:P], start=False, stop=True,
                                 skip_group_check=True).then_inc(s_tx, 1)

            def transpose_tx(L, i):
                pe.wait_ge(s_txs, L * NT + i + 1)
                transposes(tr_ps[0], txs, [s_t1])

            def dense_tx(L, i, w):
                pe.wait_ge(s_txT, L * NT + i + 1)
                dense(mm_ps, txT, w, s_d1)

            def transpose_h1(i):
                pe.wait_ge(s_h1, i + 1)
                transposes(tr_ps[1], hid1, [s_t2])

            def dense_h1(i):
                pe.wait_ge(s_h1T, i + 1)
                dense(mm_ps, hidT, wC, s_d2)

            def step(L, i, u):
                slots(L, i, u, range(0, 3))
                transpose_tx(L, i - 1)
                slots(L, i, u, range(3, 6))
                if L == 0:
                    pe.wait_ge(s_acc2, i)
                    dense_tx(L, i - 1, wB)
                    slots(L, i, u, range(6, 15))
                    transpose_h1(i - 1)
                    slots(L, i, u, range(15, SLOTS))
                    close(L, i, u)
                    dense_h1(i - 1)
                else:
                    pe.wait_ge(s_fin, i)
                    dense_tx(L, i - 1, wA)
                    slots(L, i, u, range(6, SLOTS))
                    close(L, i, u)

            pe.wait_ge(s_acc, NT + 2)
            pe.wait_ge(s_wB, 16)
            pe.wait_ge(s_wC, 16)
            for L in range(2):
                if L == 1:
                    pe.wait_ge(s_wD, 16)
                    pe.wait_ge(s_acc2, NT + 1)
                slots(L, 0, 0, range(SLOTS))
                close(L, 0, 0)
                with pe.Fori(0, NT // 2 - 1) as k:
                    step(L, 2 * k + 1, 1)
                    step(L, 2 * k + 2, 0)
                step(L, NT - 1, 1)
                transpose_tx(L, NT - 1)
                if L == 0:
                    pe.wait_ge(s_acc2, NT)
                    dense_tx(L, NT - 1, wB)
                    transpose_h1(NT - 1)
                    dense_h1(NT - 1)
                else:
                    pe.wait_ge(s_fin, NT)
                    dense_tx(L, NT - 1, wA)


_INS = ['x', 'src', 'dst', 'L0_gnn_W1_0', 'L0_gnn_W1_1', 'L0_gnn_b1', 'L0_gnn_gamma', 'L0_gnn_beta',
        'L0_gnn_W2_0', 'L0_gnn_W2_1', 'L0_gnn_b2']


def kernel(**inputs):
    import numpy as _np
    import concourse.bacc as _bacc
    from concourse import mybir as _mybir
    from concourse.bass_utils import run_bass_kernel_spmd as _run

    nc = _bacc.Bacc("TRN2", target_bir_lowering=False, num_devices=1)
    arrays, args = {}, []
    for name in _INS:
        a = _np.ascontiguousarray(inputs[name])
        arrays[f"in_{name}_dram"] = a
        args.append(nc.dram_tensor(f"in_{name}_dram", a.shape, _mybir.dt.from_np(a.dtype), kind="ExternalInput").ap())
    shape = inputs['x'].shape
    args.append(nc.dram_tensor("out_0_dram", shape, _mybir.dt.from_np(_np.dtype("float32")),
                               kind="ExternalOutput").ap())
    gnn_kernel(nc, *args)
    r = _run(nc, [arrays], core_ids=[0])
    return r.results[0]["out_0_dram"]
```

```python
from contextlib import ExitStack

import concourse.bass as bass
from concourse import mybir

F32 = mybir.dt.float32
F32R = mybir.dt.float32r
I32 = mybir.dt.int32
U32 = mybir.dt.uint32
BF16 = mybir.dt.bfloat16
ALU = mybir.AluOpType
ACT = mybir.ActivationFunctionType
AX_X = mybir.AxisListType.X

P = 128
EPS = 1e-5
SLOPE = 0.01


class Count:

    def __init__(self, sem, base=0):
        self.sem, self.base, self.n = sem, base, 0

    def add(self, instruction):
        instruction.then_inc(self.sem, 1)
        self.n += 1

    def settle(self, engine):
        engine.wait_ge(self.sem, self.base + self.n)


def gnn_kernel(nc, x, src, dst, W10, W11, b1, gamma, beta, W20, W21, b2, out):
    N, D = x.shape
    E = src.shape[0]
    KC = D // P
    TR = 125
    NT = N // TR
    TA = 112
    IN = 32
    GJ = 5
    NG = NT // GJ
    SLOTS = 17
    CAP = SLOTS * P
    GW = 4
    SPLIT = ((0, 1, 2, 3, 4, 6, 7, 8, 9, 14, 15, 16), (3, 7, 11, 15))
    SR = (4, 2)
    assert all(len(SPLIT[L]) % SR[L] == 0 for L in range(2))
    EP = 125
    EC = E // EP
    NA = NT // 2
    GA = NA // GJ
    HC = 16
    HH = EC // (HC * NA)
    TILE_SHIFT = 22
    TILE_MUL = -(-2**TILE_SHIFT // TR)
    assert NT * TR == N and NT == GJ * NG and EP * EC == E and HC * HH * NA == EC and HH == 2 and NT == 2 * NA
    for node in range(N):
        exact = node * TILE_MUL
        for near in (exact * (1 - 2.0**-23), exact * (1 + 2.0**-23)):
            assert int(near) >> TILE_SHIFT == node // TR and near < 2**31

    table = [nc.dram_tensor(f"table{n}", [N, D], F32, kind="Internal").ap() for n in range(2)]

    ctx = ExitStack()
    with ctx:
        def sb(name, shape, dt=F32):
            return ctx.enter_context(nc.sbuf_tensor(name, shape, dt))

        def sem(name):
            return ctx.enter_context(nc.semaphore(name))

        acc = sb("acc", [P, NT * D])
        rows = sb("rows", [P, SLOTS, D])
        hots = sb("hots", [P, SLOTS * P], F32R)
        high = [sb(f"high{b}", [P, D], F32R) for b in range(SR[1])]
        low = [sb(f"low{b}", [P, D], F32R) for b in range(SR[1])]
        wB = sb("wB", [P, KC, D])
        wC = sb("wC", [P, KC, D])
        bias = sb("bias", [P, D])
        gam = sb("gam", [P, D])
        bet = sb("bet", [P, D])
        ident = sb("ident", [P, P])
        iota_f = sb("iota_f", [P, P])
        part_i = sb("part_i", [P, 1], I32)
        part_f = sb("part_f", [P, 1])
        base_i = sb("base_i", [P, NT], I32)
        base_f = sb("base_f", [P, NT])
        idx_all = sb("idx_all", [P, NT * SLOTS], I32)
        loc_all = sb("loc_all", [P, NT * SLOTS])
        idx_now = sb("idx_now", [P, 2, SLOTS], I32)
        loc_now = sb("loc_now", [P, 2, SLOTS])
        src_i = sb("src_i", [EP, EC], I32)
        dst_f = sb("dst_f", [EP, EC])
        work = sb("work", [P, 5, D])
        rstd_all = sb("rstd_all", [P, NT])
        nmr_all = sb("nmr_all", [P, NT])
        dinv = sb("dinv", [P, NT])
        ndinv = sb("ndinv", [P, NT])
        ones = sb("ones", [P, 1])
        zeros_b = sb("zeros_b", [P, P], BF16)
        stats = sb("stats", [P, GJ, 6])
        mv = sb("mv", [P, GJ, 2])
        veps = sb("veps", [P, GJ])
        std = sb("std", [P, GJ])
        nxt_i = sb("nxt_i", [EP, 1], I32)
        viol = sb("viol", [EP, 2])
        row_no = sb("row_no", [NT, 4])
        row_i = sb("row_i", [NT, 1], I32)
        flag_f = sb("flag_f", [1, 1])
        flag_i = sb("flag_i", [1, 1], I32)
        gen_idx = sb("gen_idx", [EP, 1], I32)
        gen_loc = sb("gen_loc", [EP, 1])
        gen_hot = sb("gen_hot", [EP, P])

        with nc.sbuf_tensor("wA", [P, KC, D], F32) as wA:
            pass
        high += [sb(f"high{b}", [P, D], F32R) for b in range(SR[1], SR[0])]
        low += [sb(f"low{b}", [P, D], F32R) for b in range(SR[1], SR[0])]

        txs = hid = work[:, 0, :]
        txT = hidT = work[:, 1, :]
        xin, stage = work[:, 2, :], work[:, 3, :]
        gen_rows = work[0:EP, 4, :]

        small = work[:, 0:2, :].rearrange("p a b -> p (a b)").rearrange("p (n c) -> p n c", c=64)
        scale2, bias2, deg1, sqdeg, hasdeg = (small[:, n, 0:NT] for n in range(5))
        before = small[0:EP, 5, 0:NT]
        row_a, row_b = small[0:1, 6, 0:NT], small[0:1, 7, 0:NT]
        first_row = small[0:1, 8, 0:NT + 1]
        flags = small[0:1, 10, 0:1]
        start_i = small[0:1, 9, 0:NT].bitcast(I32)
        iota_i = work[:, 4, 0:P].bitcast(I32)

        xr = rows[:, 0:GJ, :]
        hr = rows[:, GJ:2 * GJ, :]
        old = rows[:, 2 * GJ:3 * GJ, :]
        new = rows[:, 3 * GJ:3 * GJ + 2, :]
        ids_b = wB[:, 0:2, :].rearrange("p a b -> p (a b)").bitcast(BF16)[0:EP, :]
        r_b, q_b = ids_b[:, 0:EC], ids_b[:, EC:2 * EC]
        picked_i = wB[:, 2:4, :].rearrange("p a b -> p (a b)").bitcast(I32)[0:NT, 0:EC]
        picked = wC[:, 2:4, :].rearrange("p a b -> p (a b)")[0:NT, 0:EC]
        qhot = wC[:, 0:2, :].rearrange("p a b -> p (a b)").bitcast(BF16)[0:EP, 0:2 * NT * HC].rearrange(
            "p (u n c) -> p u n c", u=2, c=HC)
        rhots_view = rows[:, 2 * GJ:2 * GJ + 4, :].rearrange("p a b -> p (a b)").bitcast(BF16)
        rhot = rhots_view[0:EP, 0:2 * TR * HC].rearrange("p (u n c) -> p u n c", u=2, c=HC)
        iota_n = rows[:, 2 * GJ + 4:2 * GJ + 6, :].rearrange("p a b -> p (a b)").bitcast(BF16)[
            0:EP, 0:TR * HC].rearrange("p (n c) -> p n c", c=HC)
        tmp1 = rows[:, 2 * GJ + 2:2 * GJ + 4, :].rearrange("p a b -> p (a b)").bitcast(I32)[0:EP, 0:EC]
        dst_i = rows[:, 2 * GJ:2 * GJ + 2, :].rearrange("p a b -> p (a b)").bitcast(I32)[0:EP, 0:EC]
        sortcmp = wC[:, 2:4, :].rearrange("p a b -> p (a b)")[0:EP, 0:EC]
        dst_all = loc_all[:, :].bitcast(I32)
        hT = [xin, stage]

        ps = [ctx.enter_context(nc.psum_tensor(f"ps{n}", [P, 512], F32)) for n in range(7)]
        dense_ps, tr_ps, hist_ps, misc_ps = [ps[0], ps[1]], [ps[2], ps[3]], ps[5], ps[6]
        tx_ps, mm_ps, mm2_ps = [ps[0], ps[1]], ps[4], ps[5]

        s_src, s_dst, s_nxt = sem("src_in"), sem("dst_in"), sem("nxt_in")
        s_wA, s_wB, s_wC, s_wD = sem("w10_in"), sem("w11_in"), sem("w20_in"), sem("w21_in")
        s_b1, s_b2, s_gb = sem("b1_in"), sem("b2_in"), sem("gamma_beta_in")
        s_iota = sem("iota_done")
        s_const = sem("constants_done")
        s_setup = sem("setup_steps")
        s_x = [sem(f"x_in{j}") for j in range(GJ)]
        s_aggr = sem("stats_steps")
        s_var, s_std, s_norm = sem("var_ready"), sem("std_ready"), sem("norm_ready")
        s_h = sem("h_ready")
        s_tr = sem("hT_in_psum")
        s_hT = sem("hT_ready")
        s_dense = sem("dense_ready")
        s_acc = sem("acc_stored")
        s_hhot, s_hist = sem("hist_hots_ready"), sem("hist_hots_used")
        s_histend = sem("hist_ready")
        s_post = sem("post_steps")
        s_deg1, s_sqdeg = sem("deg_ready"), sem("sqrt_deg_ready")
        s_before, s_rows, s_rowno, s_picked = (sem("before_ready"), sem("row_counts_in_psum"),
                                               sem("row_no_ready"), sem("picked_rows_in"))
        s_viol, s_stats = sem("viol_ready"), sem("tile_stats_ready")
        s_first, s_starts = sem("first_ready"), sem("starts_in_psum")
        s_startok = sem("start_index_ready")
        s_scale2 = sem("scale2_ready")
        s_flag = sem("flag_ready")
        s_idx = sem("edge_slots_in")
        s_loc = sem("loc_ready")
        s_xo = [sem(f"old_x_in{j}") for j in range(GJ)]
        s_new, s_old = sem("new_tile_ready"), sem("old_tile_ready")
        s_tabn = [sem(f"new_tiles_out{u}") for u in range(2)]
        s_tabo = [sem(f"old_tile_out{j}") for j in range(GJ)]
        s_gath = [sem(f"slot_rows_in{c}") for c in range(SLOTS)]
        s_pass, s_dpass = sem("pool_passed"), sem("vector_passed")
        s_idxc = sem("idx_copied")
        s_locc = sem("loc_copied")
        s_hot = sem("hot_ready")
        s_slot = sem("slot_summed")
        s_tx = sem("tx_in_psum")
        s_txs = sem("txs_ready")
        s_t1, s_txT = sem("txT_in_psum"), sem("txT_ready")
        s_d1, s_mm = sem("dense1_in_psum"), sem("dense1_read")
        s_epi = sem("epilogue_steps")
        s_evar, s_estd = sem("epi_var_ready"), sem("epi_std_ready")
        s_high, s_low = sem("high_ready"), sem("low_ready")
        s_h1 = sem("h1_ready")
        s_t2, s_h1T = sem("h1T_in_psum"), sem("h1T_ready")
        s_d2 = sem("dense2_in_psum")
        s_acc2 = sem("acc2_stored")
        s_xb = sem("residual_plus_acc")
        s_xr = sem("residual_in")
        s_hs1 = sem("hs1_ready")
        s_tab1 = sem("table1_out")
        s_fin = sem("out_ready")
        s_out = sem("out_out")
        s_greset = sem("gen_rows_in_reset")
        s_gidx, s_ggath, s_gloc, s_ghot, s_gmm = (sem("gen_idx_copied"), sem("gen_rows_in"),
                                                  sem("gen_loc_ready"), sem("gen_hot_ready"),
                                                  sem("gen_slot_summed"))

        block = ctx.enter_context(nc.Block())

        def acc_of(t):
            return acc[:, bass.ds(t * D, D)]

        def col(a, t):
            return a[:, bass.ds(t, 1)]

        def split_no(L, i, c):
            return L * NT * len(SPLIT[0]) + i * len(SPLIT[L]) + SPLIT[L].index(c)

        def buffer_of(L, c):
            return SPLIT[L].index(c) % SR[L]

        def last_use(L, i, c):
            s = SPLIT[L].index(c) - SR[L]
            before = SPLIT[L][s] + (SLOTS if s >= 0 else 0)
            return (L * NT + i) * SLOTS + before + 1

        TABLE_ORDER = (("new", 0), ("old", 0), ("new", 1), ("old", 1), ("new", 2), ("old", 2),
                       ("new", 3), ("new", 4), ("old", 3), ("old", 4))

        K_EPI = 5

        @block.sync
        def _(sp):
            def rows_of(array, t, n0, n1):
                return array[bass.ds(t * TR + n0, n1 - n0), :]

            def load_tile(target, array, t, s):
                for n0, n1 in ((0, TA), (TA, TR)):
                    sp.dma_start(target[n0:n1, :], rows_of(array, t, n0, n1)).then_inc(s, 16)

            def store_tile(array, t, source, s):
                for n0, n1 in ((0, TA), (TA, TR)):
                    sp.dma_start(rows_of(array, t, n0, n1), source[n0:n1, :]).then_inc(s, 16)

            sp.dma_start(dst_i, dst.rearrange("(p c) -> p c", p=EP)).then_inc(s_dst, 16)
            sp.dma_start(src_i[:, :], src.rearrange("(p c) -> p c", p=EP)).then_inc(s_src, 16)
            sp.wait_ge(s_setup, 2)
            for j in range(GJ):
                load_tile(xr[:, j, :], x, j, s_x[j])
            sp.dma_start(wA[:, :, :], W10.rearrange("(k p) n -> p k n", p=P)).then_inc(s_wA, 16)
            sp.dma_start(bias[:, :], b1.partition_broadcast(P)).then_inc(s_b1, 16)
            with nc.allow_non_contiguous_dma(reason="first edge of each row of the edge list"):
                sp.dma_start(nxt_i[0:EP - 1, :],
                             dst[EC:E].rearrange("(p c) -> p c", c=EC)[:, 0:1]).then_inc(s_nxt, 16)
            sp.dma_start(gam[:, :], gamma.partition_broadcast(P)).then_inc(s_gb, 16)
            sp.dma_start(bet[:, :], beta.partition_broadcast(P)).then_inc(s_gb, 16)

            with sp.Fori(0, GA) as g:
                for j in range(GJ):
                    t = g * GJ + j
                    sp.wait_ge(s_h, t + 1)
                    load_tile(xr[:, j, :], x, t + GJ, s_x[j])
                sp.wait_ge(s_startok, 1)
                for j in range(2 * GJ):
                    i = g * 2 * GJ + j
                    first = sp.value_load(start_i[0:1, bass.ds(i, 1)], min_val=0, max_val=E - CAP)
                    sp.dma_start(idx_all[:, bass.ds(i * SLOTS, SLOTS)],
                                 src[bass.ds(first, CAP)].rearrange("(p c) -> p c", p=P)).then_inc(s_idx, 16)
                    sp.dma_start(dst_all[:, bass.ds(i * SLOTS, SLOTS)],
                                 dst[bass.ds(first, CAP)].rearrange("(p c) -> p c", p=P)).then_inc(s_idx, 16)

            sp.wait_ge(s_histend, 1)

            def second_half(g, first=False, more=True):
                for j in range(GJ):
                    t = g * GJ + j
                    if not first:
                        sp.wait_ge(s_tabo[j], 16 * (g - GA))
                    load_tile(old[:, j, :], x, t - NA, s_xo[j])
                    if more:
                        sp.wait_ge(s_new, t - NA + 1)
                        load_tile(xr[:, j, :], x, t + GJ, s_x[j])

            second_half(GA, first=True)
            with sp.Fori(GA + 1, NG - 1) as g:
                second_half(g)
            second_half(NG - 1, more=False)

            sp.dma_start(wB[:, :, :], W11.rearrange("(k p) n -> p k n", p=P)).then_inc(s_wB, 16)
            sp.dma_start(wC[:, :, :], W20.rearrange("(k p) n -> p k n", p=P)).then_inc(s_wC, 16)
            sp.wait_ge(s_acc, NT + 2)
            sp.dma_start(bias[:, :], b2.partition_broadcast(P)).then_inc(s_b2, 16)

            load_tile(xin, x, 0, s_xr)
            with sp.Fori(0, NT) as i:
                sp.wait_ge(s_hs1, i + 1)
                store_tile(table[1], i, stage, s_tab1)

            sp.wait_ge(s_mm, NT + 1)
            sp.dma_start(wA[:, :, :], W21.rearrange("(k p) n -> p k n", p=P)).then_inc(s_wD, 16)

            def layer2_io(i, load=True):
                sp.wait_ge(s_fin, i + 2)
                store_tile(out, i, stage, s_out)
                if load:
                    load_tile(xin, x, i + 1, s_xr)

            with sp.Fori(0, NT - 1) as i:
                layer2_io(i)
            layer2_io(NT - 1, load=False)
            sp.wait_ge(s_out, IN * (NT + 1))

        @block.gpsimd
        def _(pool):
            nc.gpsimd.iota(iota_i[:, :], pattern=[[1, P]], base=0, channel_multiplier=0).then_inc(s_iota, 1)
            nc.gpsimd.iota(part_i[:, :], pattern=[[1, 1]], base=0, channel_multiplier=1).then_inc(s_iota, 1)
            nc.gpsimd.iota(base_i[:, :], pattern=[[TR, NT]], base=0, channel_multiplier=0).then_inc(s_iota, 1)

            pool.wait_ge(s_rowno, 1)
            pool.sem_inc(s_pass, 1)
            nc.gpsimd.indirect_dma_start(
                out=picked_i[:, :], out_offset=None, in_=dst.rearrange("(p c) -> p c", p=EP),
                in_offset=bass.IndirectOffsetOnAxis(ap=row_i[:, 0:1].bitcast(U32), axis=0),
            ).then_inc(s_picked, 16)

            def store_table(array, t, s):
                pool.sem_inc(s_pass, 1)
                pool.dma_start(table[0][bass.ds(t * TR, TR), :], array[0:TR, :]).then_inc(s, 16)

            with pool.Fori(GA, NG) as g:
                for kind, j in TABLE_ORDER:
                    t = g * GJ + j
                    if kind == "new":
                        pool.wait_ge(s_new, t - NA + 1)
                        store_table(new[:, j % 2, :], t, s_tabn[j % 2])
                    else:
                        pool.wait_ge(s_old, t - NA + 1)
                        store_table(old[:, j, :], t - NA, s_tabo[j])

            bad = {}

            def gather_tile(L, i, u):
                n = L * NT + i
                pool.wait_ge(s_slot, n * SLOTS + 1)
                pool.wait_ge(s_idxc, n + 1)
                pool.sem_inc(s_pass, 1)
                for c in range(SLOTS):
                    if c % GW == 1:
                        pool.wait_ge(s_slot, n * SLOTS + min(c + GW, SLOTS))
                        pool.sem_inc(s_pass, 1)
                    nc.gpsimd.indirect_dma_start(
                        out=rows[:, c, :], out_offset=None, in_=table[L][:, :],
                        in_offset=bass.IndirectOffsetOnAxis(ap=idx_now[:, u, c:c + 1].bitcast(U32), axis=0),
                    ).then_inc(s_gath[c], 16)
                with pool.If(bad["pool"] > 0):
                    with pool.Fori(0, EC) as e:
                        m = n * EC + e
                        pool.wait_ge(s_gmm, m + 1)
                        nc.gpsimd.tensor_copy(gen_idx[:, :], src_i[:, bass.ds(e, 1)]).then_inc(s_gidx, 1)
                        pool.wait_ge(s_gidx, m + 1)
                        pool.sem_inc(s_pass, 1)
                        nc.gpsimd.indirect_dma_start(
                            out=gen_rows, out_offset=None, in_=table[L][:, :],
                            in_offset=bass.IndirectOffsetOnAxis(ap=gen_idx[:, 0:1].bitcast(U32), axis=0),
                        ).then_inc(s_ggath, 16)
                    pool.wait_ge(s_gmm, (n + 1) * EC + 1)
                    pool.sem_inc(s_pass, 1)
                    nc.gpsimd.inc_swdge_sem([s_ggath], [16 * EC], mode="sub")
                    pool.sem_inc(s_greset, 1)

            pool.wait_ge(s_flag, 1)
            bad["pool"] = pool.value_load(flag_i[0:1, 0:1], min_val=0, max_val=1)
            pool.wait_ge(s_loc, 1)
            pool.wait_ge(s_tr, NT + GJ)
            for u in range(2):
                pool.wait_ge(s_tabn[u], 16 * (NG - GA) * (3 - u))
            for j in range(GJ):
                pool.wait_ge(s_tabo[j], 16 * (NG - GA))
            for L in range(2):
                if L == 1:
                    pool.wait_ge(s_tab1, IN * (NT + 1))
                with pool.Fori(0, NT // 2) as k:
                    gather_tile(L, 2 * k, 0)
                    gather_tile(L, 2 * k + 1, 1)

        @block.scalar
        def _(act):
            def take_stds(g):
                act.wait_ge(s_var, g + 1)
                nc.scalar.activation(std[:, :], veps[:, :], ACT.Sqrt).then_inc(s_std, 1)

            def make_h(g, j):
                t = g * GJ + j
                act.wait_ge(s_x[j], IN * (g + 1))
                act.wait_ge(s_norm, g + 1)
                act.wait_ge(s_tr, t + 1)
                nc.scalar.activation(hr[:, j, :], xr[:, j, :], ACT.Relu, bias=col(nmr_all, t),
                                     scale=col(rstd_all, t)).then_inc(s_h, 1)

            def copy_hT(g, j):
                t = g * GJ + j
                act.wait_ge(s_tr, t + 1 + GJ)
                act.wait_ge(s_dense, t + 2 if j == 0 else t + 1)
                nc.scalar.copy(hT[j % 2], tr_ps[j % 2][:, :]).then_inc(s_hT, 1)

            def make_new(g, j, first):
                t = g * GJ + j
                act.wait_ge(s_scale2, g - GA + 2)
                if not first or j >= 2:
                    act.wait_ge(s_tabn[j % 2], 16 * ((g - GA) * (3 - j % 2) + j // 2))
                nc.scalar.activation(new[:, j % 2, :], xr[:, j, :], ACT.Relu, bias=col(bias2, t),
                                     scale=col(scale2, t)).then_inc(s_new, 1)

            def make_old(g, j):
                t = g * GJ + j
                act.wait_ge(s_xo[j], IN * (g - GA + 1))
                nc.scalar.activation(old[0:TR, j, :], old[0:TR, j, :], ACT.Relu, bias=col(bias2, t - NA)[0:TR, :],
                                     scale=col(scale2, t - NA)[0:TR, :]).then_inc(s_old, 1)

            take_stds(0)
            with act.Fori(0, GA) as g:
                make_h(g, 0)
                make_h(g, 1)
                copy_hT(g, 0)
                make_h(g, 2)
                make_h(g, 3)
                copy_hT(g, 1)
                make_h(g, 4)
                for j in range(2, GJ):
                    copy_hT(g, j)
                take_stds(g + 1)

            act.wait_ge(s_deg1, 1)
            nc.scalar.activation(sqdeg[:, :], deg1[:, :], ACT.Sqrt).then_inc(s_sqdeg, 1)

            def second_half(g, first=False, more=True):
                make_h(g, 0)
                make_h(g, 1)
                copy_hT(g, 0)
                for j in range(3):
                    make_new(g, j, first)
                    make_h(g, j + 2)
                    make_old(g, j)
                    copy_hT(g, j + 1)
                make_new(g, 3, first)
                make_new(g, 4, first)
                copy_hT(g, 4)
                make_old(g, 3)
                make_old(g, 4)
                if more:
                    take_stds(g + 1)

            second_half(GA, first=True)
            with act.Fori(GA + 1, NG - 1) as g:
                second_half(g)
            second_half(NG - 1, more=False)

            def copy_idx(L, i, u):
                if L or not isinstance(i, int):
                    act.wait_ge(s_slot, (L * NT + i) * SLOTS)
                nc.scalar.copy(idx_now[:, u, :], idx_all[:, bass.ds(i * SLOTS, SLOTS)]).then_inc(s_idxc, 1)

            def make_high(L, i, which):
                for c in which:
                    act.wait_ge(s_slot, last_use(L, i, c))
                    act.wait_ge(s_gath[c], 16 * (L * NT + i + 1))
                    nc.scalar.copy(high[buffer_of(L, c)][:, :], rows[:, c, :]).then_inc(s_high, 1)

            def take_tx(L, i, u):
                n = L * NT + i
                act.wait_ge(s_tx, n + 1)
                act.wait_ge(s_t1, n + 1)
                if L == 0:
                    act.wait_ge(s_t2, i + 1)
                nc.scalar.activation(txs, tx_ps[u][:, :], ACT.Copy, scale=col(ndinv, i)).then_inc(s_txs, 1)

            def copy_txT(L, i):
                n = L * NT + i
                act.wait_ge(s_t1, n + 2)
                act.wait_ge(s_d1, n + 1)
                if L == 0:
                    act.wait_ge(s_d2, i + 1)
                nc.scalar.copy(txT, tr_ps[0][:, :]).then_inc(s_txT, 1)

            def take_std(i):
                act.wait_ge(s_evar, i + 1)
                nc.scalar.activation(std[:, 0:1], veps[:, 0:1], ACT.Sqrt).then_inc(s_estd, 1)

            def make_hs1(i):
                act.wait_ge(s_h1, i + 1)
                act.wait_ge(s_tab1, IN * (i + 1))
                nc.scalar.activation(stage, hid, ACT.Copy, scale=col(dinv, i)).then_inc(s_hs1, 1)

            def copy_hidT(i):
                act.wait_ge(s_t2, i + 2)
                nc.scalar.copy(hidT, tr_ps[1][:, :]).then_inc(s_h1T, 1)

            def store_acc2(i):
                act.wait_ge(s_d2, i + 2)
                nc.scalar.copy(acc_of(i), mm2_ps[:, :]).then_inc(s_acc2, 1)

            def act_step(L, i, u, prev=True, prev2=True, more=True):
                def highs(first, end):
                    make_high(L, i, [c for c in SPLIT[L] if first <= c < end])

                if L == 0:
                    highs(0, 3)
                    if prev:
                        take_tx(L, i - 1, 1 - u)
                    highs(3, 4)
                    if more:
                        copy_idx(L, i + 1, 1 - u)
                    highs(4, 5)
                    if prev2:
                        store_acc2(i - 2)
                    highs(5, 7)
                    if prev:
                        copy_txT(L, i - 1)
                    highs(7, 10)
                    if prev:
                        take_std(i - 1)
                    highs(10, 16)
                    if prev:
                        make_hs1(i - 1)
                    highs(16, SLOTS)
                    if prev:
                        copy_hidT(i - 1)
                else:
                    if prev:
                        take_tx(L, i - 1, 1 - u)
                    if more:
                        copy_idx(L, i + 1, 1 - u)
                    highs(0, 4)
                    if prev:
                        copy_txT(L, i - 1)
                    highs(4, SLOTS)

            act.wait_ge(s_loc, 1)
            for L in range(2):
                copy_idx(L, 0, 0)
                if L == 1:
                    act.wait_ge(s_t2, NT + 1)
                    act.wait_ge(s_d2, NT + 1)
                act_step(L, 0, 0, prev=False, prev2=False)
                act_step(L, 1, 1, prev2=False)
                with act.Fori(1, NT // 2 - 1) as k:
                    act_step(L, 2 * k, 0)
                    act_step(L, 2 * k + 1, 1)
                act_step(L, NT - 2, 0)
                act_step(L, NT - 1, 1, more=False)
                take_tx(L, NT - 1, 1)
                copy_txT(L, NT - 1)
                if L == 0:
                    store_acc2(NT - 2)
                    take_std(NT - 1)
                    make_hs1(NT - 1)
                    copy_hidT(NT - 1)
                    store_acc2(NT - 1)

        @block.vector
        def _(dve):
            own = Count(s_setup)
            dve.sem_inc(s_tr, GJ)
            dve.sem_inc(s_dense, 2)
            dve.sem_inc(s_hT, 2)
            dve.sem_inc(s_acc, 2)
            dve.sem_inc(s_hist, 2)
            dve.sem_inc(s_slot, SLOTS)
            dve.sem_inc(s_t1, 1)
            dve.sem_inc(s_d1, 1)
            dve.sem_inc(s_d2, 1)
            dve.sem_inc(s_t2, 1)
            dve.sem_inc(s_acc2, 1)
            dve.sem_inc(s_fin, 1)
            dve.sem_inc(s_mm, 1)
            dve.sem_inc(s_gmm, 1)
            dve.sem_inc(s_greset, 1)
            dve.sem_inc(s_tab1, IN)
            dve.sem_inc(s_out, IN)
            own.add(nc.vector.memset(xr[96:P, :, :], 0.0))
            own.add(nc.vector.memset(nxt_i[:, :], N))
            own.add(nc.vector.memset(ones[:, :], 1.0))
            own.add(nc.vector.memset(zeros_b[:, :], 0.0))
            dve.wait_ge(s_iota, 3)
            own.add(nc.vector.tensor_copy(iota_f[:, :], iota_i[:, :]))
            own.add(nc.vector.tensor_copy(part_f[:, :], part_i[:, :]))
            own.add(nc.vector.tensor_copy(base_f[:, :], base_i[:, :]))
            own.settle(dve)
            own.add(nc.vector.tensor_scalar(ident[:, :], iota_f[:, :], part_f[:, 0:1], None, ALU.is_equal))
            own.settle(dve)
            nc.vector.tensor_copy(flag_f[:, :], ones[0:1, 0:1]).then_inc(s_const, 1)

            def search_rows():
                dve.wait_ge(s_dst, 16)
                own.add(nc.vector.tensor_copy(dst_f[:, :], dst_i))
                own.settle(dve)
                nc.vector.tensor_scalar(before[:, :], base_f[0:EP, :], dst_f[:, 0:1], None,
                                        ALU.is_gt).then_inc(s_before, 1)
                dve.wait_ge(s_rows, 1)
                own.add(nc.vector.tensor_scalar(row_no[:, 0:1], misc_ps[0:NT, 0:1], -1.0, 0.0, ALU.add, ALU.max))
                own.settle(dve)
                nc.vector.tensor_copy(row_i[:, :], row_no[:, 0:1]).then_inc(s_rowno, 1)

            def edge_ids():
                dve.wait_ge(s_src, 16)
                own.add(nc.vector.tensor_scalar(tmp1, src_i[:, :], float(TILE_MUL), None, ALU.mult))
                own.settle(dve)
                own.add(nc.vector.tensor_single_scalar(tmp1, tmp1, TILE_SHIFT, ALU.logical_shift_right))
                own.settle(dve)
                own.add(nc.vector.tensor_copy(q_b, tmp1))
                own.add(nc.vector.scalar_tensor_tensor(out=r_b, in0=tmp1, scalar=-float(TR), in1=src_i[:, :],
                                                       op0=ALU.mult, op1=ALU.add))
                own.add(nc.vector.tensor_copy(iota_n, iota_f[0:EP, 0:TR].unsqueeze(2).to_broadcast([EP, TR, HC])))
                own.settle(dve)

            def order():
                dve.wait_ge(s_nxt, 16)
                own.add(nc.vector.tensor_copy(viol[:, 1:2], nxt_i[:, :]))
                own.add(nc.vector.tensor_tensor(sortcmp[:, 0:EC - 1], dst_f[:, 0:EC - 1], dst_f[:, 1:EC], ALU.is_gt))
                own.settle(dve)
                own.add(nc.vector.tensor_tensor(sortcmp[:, EC - 1:EC], dst_f[:, EC - 1:EC], viol[:, 1:2], ALU.is_gt))
                own.settle(dve)
                nc.vector.reduce_max(viol[:, 0:1], sortcmp, AX_X).then_inc(s_viol, 1)

            def search_within():
                dve.wait_ge(s_picked, 16)
                own.add(nc.vector.tensor_copy(picked[:, :], picked_i[:, :]))
                own.add(nc.vector.tensor_scalar(row_no[:, 1:2], part_f[0:NT, :], float(TR), None, ALU.mult))
                own.settle(dve)
                own.add(nc.vector.tensor_scalar(picked[:, :], picked[:, :], row_no[:, 1:2], None, ALU.is_lt))
                own.settle(dve)
                own.add(nc.vector.reduce_sum(row_no[:, 2:3], picked[:, :], AX_X))
                own.settle(dve)
                nc.vector.scalar_tensor_tensor(out=row_no[:, 3:4], in0=row_no[:, 0:1], scalar=float(EC),
                                               in1=row_no[:, 2:3], op0=ALU.mult, op1=ALU.add).then_inc(s_first, 1)

            def start_rows():
                dve.wait_ge(s_starts, 1)
                own.add(nc.vector.tensor_copy(first_row[:, 0:NT], misc_ps[0:1, 64:64 + NT]))
                own.add(nc.vector.memset(first_row[:, NT:NT + 1], float(E)))
                own.add(nc.vector.tensor_copy(flag_f[:, :], misc_ps[0:1, 128:129]))
                own.settle(dve)
                own.add(nc.vector.tensor_scalar_min(row_a[:, :], first_row[:, 0:NT], float(E - CAP)))
                own.settle(dve)
                nc.vector.tensor_copy(start_i[:, :], row_a[:, :]).then_inc(s_startok, 1)
                own.add(nc.vector.tensor_tensor(row_b[:, :], first_row[:, 1:NT + 1], row_a[:, :], ALU.subtract))
                own.settle(dve)
                own.add(nc.vector.tensor_scalar(row_b[:, :], row_b[:, :], float(CAP), None, ALU.is_gt))
                own.settle(dve)
                own.add(nc.vector.reduce_max(flags[:, :], row_b[:, :], AX_X))
                own.settle(dve)
                own.add(nc.vector.tensor_tensor(flag_f[:, :], flag_f[:, :], flags[:, :], ALU.max))
                own.settle(dve)
                own.add(nc.vector.tensor_scalar(flag_f[:, :], flag_f[:, :], 0.0, None, ALU.is_gt))
                own.settle(dve)
                nc.vector.tensor_copy(flag_i[:, :], flag_f[:, :]).then_inc(s_flag, 1)

            def hist_hots(t):
                for v in range(HH):
                    m = t * HH + v
                    columns = bass.ds(m * HC, HC)
                    dve.wait_ge(s_hist, m + 1)
                    nc.vector.tensor_tensor(rhot[:, v], iota_n, r_b[:, columns].unsqueeze(1).to_broadcast([EP, TR, HC]),
                                            ALU.is_equal).then_inc(s_hhot, 1)
                    nc.vector.tensor_tensor(qhot[:, v], iota_n[:, 0:NT, :],
                                            q_b[:, columns].unsqueeze(1).to_broadcast([EP, NT, HC]),
                                            ALU.is_equal).then_inc(s_hhot, 1)

            def stats_of(g, j):
                dve.wait_ge(s_x[j], IN * (g + 1))
                nc.vector.bn_stats(stats[:, j, :], xr[:, j, :]).then_inc(s_stats, 1)

            def group_var(g):
                dve.wait_ge(s_stats, GJ * (g + 1))
                dve.sem_inc(s_dpass, 1)
                for j in range(GJ):
                    last = nc.vector.bn_aggr(mv[:, j, :], stats[:, j, :])
                last.then_inc(s_aggr, 1)
                dve.wait_ge(s_aggr, 2 * g + 1)
                nc.vector.tensor_scalar_add(veps[:, :], mv[:, :, 1], EPS).then_inc(s_var, 1)

            def group_norm(g):
                dve.wait_ge(s_std, g + 1)
                nc.vector.reciprocal(rstd_all[:, bass.ds(g * GJ, GJ)], std[:, :]).then_inc(s_aggr, 1)
                dve.wait_ge(s_aggr, 2 * g + 2)
                nc.vector.scalar_tensor_tensor(out=nmr_all[:, bass.ds(g * GJ, GJ)], in0=mv[:, :, 0], scalar=-1.0,
                                               in1=rstd_all[:, bass.ds(g * GJ, GJ)], op0=ALU.mult,
                                               op1=ALU.mult).then_inc(s_norm, 1)

            def store_acc(t, j):
                dve.wait_ge(s_dense, t + 3)
                nc.vector.tensor_tensor(acc_of(t), dense_ps[j % 2][:, :], bias[:, :], ALU.add).then_inc(s_acc, 1)

            def dense_group(g, hist, first=False, hist_last=False, more=True):
                for j in range(GJ):
                    t = g * GJ + j
                    if j == GJ - 1 and more:
                        group_norm(g + 1)
                    if hist and not (hist_last and j == GJ - 1):
                        hist_hots(t + 1)
                    if j == GJ - 1 and hist_last:
                        after_histogram()
                    store_acc(t, j)
                    if first and j == 0:
                        search_within()
                    if first and j == 1:
                        order()
                    if first and j == 2:
                        start_rows()
                    if more and j in (1, 2):
                        stats_of(g + 1, 2 * j - 2)
                        stats_of(g + 1, 2 * j - 1)
                    if more and j == 3:
                        stats_of(g + 1, 4)
                        group_var(g + 1)

            post = Count(s_post)

            def after_histogram():
                dve.wait_ge(s_histend, 1)
                nc.vector.tensor_scalar_max(deg1[:, :], hist_ps[:, 0:NT], 1.0).then_inc(s_deg1, 1)
                post.add(nc.vector.tensor_scalar(hasdeg[:, :], hist_ps[:, 0:NT], 0.0, None, ALU.is_gt))
                dve.wait_ge(s_sqdeg, 1)
                post.add(nc.vector.reciprocal(dinv[:, :], sqdeg[:, :]))
                post.settle(dve)
                post.add(nc.vector.tensor_tensor(dinv[:, :], dinv[:, :], hasdeg[:, :], ALU.mult))
                post.settle(dve)
                post.add(nc.vector.tensor_scalar_mul(ndinv[:, :], dinv[:, :], -1.0))
                scales(0, NA, GA)

            def scales(t, tiles, groups):
                these = bass.ds(t, tiles)
                dve.wait_ge(s_norm, groups)
                nc.vector.tensor_tensor(scale2[:, these], rstd_all[:, these], dinv[:, these], ALU.mult)
                nc.vector.tensor_tensor(bias2[:, these], nmr_all[:, these], dinv[:, these],
                                        ALU.mult).then_inc(s_scale2, 1)

            for j in range(GJ):
                stats_of(0, j)
            group_var(0)
            search_rows()
            group_norm(0)
            edge_ids()
            hist_hots(0)
            dve.wait_ge(s_b1, 16)
            dense_group(0, True, first=True)
            with dve.Fori(1, GA - 1) as g:
                dense_group(g, True)
            dense_group(GA - 1, True, hist_last=True)
            with dve.Fori(GA, NG - 1) as g:
                scales(g * GJ, GJ, g + 1)
                dense_group(g, False)
            scales((NG - 1) * GJ, GJ, NG)
            dense_group(NG - 1, False, more=False)

            dve.wait_ge(s_idx, 2 * 16 * NT)
            post.add(nc.vector.tensor_copy(loc_all[:, :], dst_all))
            post.settle(dve)
            loc3 = loc_all[:, :].rearrange("p (i c) -> p i c", c=SLOTS)
            nc.vector.tensor_tensor(loc3, loc3, base_f[:, :].unsqueeze(2).to_broadcast([P, NT, SLOTS]),
                                    ALU.subtract).then_inc(s_loc, 1)
            dve.wait_ge(s_loc, 1)
            dve.wait_ge(s_flag, 1)
            bad = dve.value_load(flag_i[0:1, 0:1], min_val=0, max_val=1)

            def copy_loc(L, i, u):
                dve.wait_ge(s_slot, (L * NT + i) * SLOTS + 1)
                nc.vector.tensor_copy(loc_now[:, u, :], loc_all[:, bass.ds(i * SLOTS, SLOTS)]).then_inc(s_locc, 1)
                dve.wait_ge(s_locc, L * NT + i + 1)

            def hots_of(L, i, u, first, end):
                n = L * NT + i
                for c in range(first, end):
                    dve.wait_ge(s_slot, n * SLOTS + c + 1)
                    nc.vector.tensor_scalar(hots[:, c * P:(c + 1) * P], iota_f[:, :], loc_now[:, u, c:c + 1],
                                            None, ALU.is_equal).then_inc(s_hot, 1)

            def make_low(L, i, c):
                b = buffer_of(L, c)
                dve.wait_ge(s_high, split_no(L, i, c) + 1)
                nc.vector.tensor_tensor(low[b][:, :], rows[:, c, :], high[b][:, :].bitcast(F32),
                                        ALU.subtract).then_inc(s_low, 1)

            def general(L, i):
                n = L * NT + i
                with dve.If(bad > 0):
                    with dve.Fori(0, EC) as e:
                        m = n * EC + e
                        dve.wait_ge(s_gmm, m + 1)
                        nc.vector.tensor_tensor(gen_loc[:, :], dst_f[:, bass.ds(e, 1)],
                                                base_f[0:EP, bass.ds(i, 1)], ALU.subtract).then_inc(s_gloc, 1)
                        dve.wait_ge(s_gloc, m + 1)
                        nc.vector.tensor_scalar(gen_hot[:, :], iota_f[0:EP, :], gen_loc[:, 0:1], None,
                                                ALU.is_equal).then_inc(s_ghot, 1)

            def conv_stats(i):
                own = Count(s_epi, i * K_EPI)
                dve.wait_ge(s_d1, i + 2)
                nc.vector.tensor_tensor(hid, mm_ps[:, :], acc_of(i), ALU.add).then_inc(s_mm, 1)
                dve.wait_ge(s_mm, i + 2)
                own.add(nc.vector.bn_stats(stats[:, 0, :], hid))
                own.settle(dve)
                dve.sem_inc(s_dpass, 1)
                own.add(nc.vector.bn_aggr(mv[:, 0, :], stats[:, 0, :]))
                own.settle(dve)
                nc.vector.tensor_scalar_add(veps[:, 0:1], mv[:, 0, 1:2], EPS).then_inc(s_evar, 1)
                own.add(nc.vector.scalar_tensor_tensor(out=hid, in0=hid, scalar=mv[:, 0, 0:1], in1=gam[:, :],
                                                       op0=ALU.subtract, op1=ALU.mult))
                return own

            def norm1(i, own):
                dve.wait_ge(s_estd, i + 1)
                own.add(nc.vector.reciprocal(veps[:, 1:2], std[:, 0:1]))
                own.settle(dve)
                own.add(nc.vector.scalar_tensor_tensor(out=hid, in0=hid, scalar=veps[:, 1:2], in1=bet[:, :],
                                                       op0=ALU.mult, op1=ALU.add))
                own.settle(dve)
                nc.vector.scalar_tensor_tensor(out=hid, in0=hid, scalar=SLOPE, in1=hid, op0=ALU.mult,
                                               op1=ALU.max).then_inc(s_h1, 1)
                assert own.n == K_EPI

            def finish2(i):
                dve.wait_ge(s_xr, IN * (i + 1))
                nc.vector.tensor_tensor(xin, xin, acc_of(i), ALU.add).then_inc(s_xb, 1)
                dve.wait_ge(s_xb, 2 * i + 1)
                nc.vector.tensor_tensor(xin, xin, bias[:, :], ALU.add).then_inc(s_xb, 1)
                dve.wait_ge(s_xb, 2 * i + 2)
                dve.wait_ge(s_d1, NT + i + 2)
                dve.wait_ge(s_out, IN * (i + 1))
                nc.vector.tensor_tensor(stage, mm_ps[:, :], xin, ALU.add).then_inc(s_fin, 1)

            LATE = 14

            def dve_step(L, i, u, prev=True, more=True):
                def low(*which):
                    for c in which:
                        make_low(L, i, c)

                def next_hots(first, end):
                    if more:
                        if first == 0:
                            copy_loc(L, i + 1, 1 - u)
                        hots_of(L, i + 1, 1 - u, first, end)

                if L == 0:
                    low(0, 1)
                    if prev:
                        hots_of(L, i, u, LATE, SLOTS)
                    low(2, 3)
                    next_hots(0, 1)
                    low(4)
                    next_hots(1, 2)
                    low(6, 7)
                    next_hots(2, 4)
                    low(8, 9)
                    next_hots(4, 6)
                    if prev:
                        own = conv_stats(i - 1)
                        norm1(i - 1, own)
                    low(14, 15, 16)
                    next_hots(6, LATE)
                else:
                    if prev:
                        hots_of(L, i, u, LATE, SLOTS)
                    low(3)
                    next_hots(0, 3)
                    low(7)
                    next_hots(3, 5)
                    if prev:
                        finish2(i - 1)
                    next_hots(5, 8)
                    low(11)
                    next_hots(8, 12)
                    low(15)
                    next_hots(12, LATE)
                general(L, i)

            dve.wait_ge(s_gb, 32)
            dve.wait_ge(s_b2, 16)
            for L in range(2):
                if L == 1:
                    dve.wait_ge(s_tab1, IN * (NT + 1))
                    dve.wait_ge(s_acc2, NT + 1)
                copy_loc(L, 0, 0)
                hots_of(L, 0, 0, 0, SLOTS)
                dve_step(L, 0, 0, prev=False)
                with dve.Fori(0, NT // 2 - 1) as k:
                    dve_step(L, 2 * k + 1, 1)
                    dve_step(L, 2 * k + 2, 0)
                dve_step(L, NT - 1, 1, more=False)
                if L == 0:
                    own = conv_stats(NT - 1)
                    norm1(NT - 1, own)
                else:
                    finish2(NT - 1)

        @block.tensor
        def _(pe):
            def transposes(to, source, signal):
                for k in range(KC):
                    last = nc.tensor.transpose(to[:, k * P:(k + 1) * P], source[:, k * P:(k + 1) * P], ident[:, :])
                for s in signal:
                    last.then_inc(s, 1)

            def dense(to, source, w, signal):
                for k in range(KC):
                    last = nc.tensor.matmul(to[:, :], source[:, k * P:(k + 1) * P], w[:, k, :],
                                            start=k == 0, stop=k == KC - 1)
                last.then_inc(signal, 1)

            def histogram(t):
                for v in range(HH):
                    m = t * HH + v
                    pe.wait_ge(s_hhot, 2 * m + 2)
                    for c in range(HC):
                        last = nc.tensor.matmul(hist_ps[0:TR, 0:NT], rhot[:, v, :, c], qhot[:, v, :, c],
                                                start=False, stop=False)
                    last.then_inc(s_hist, 1)

            def transpose_h(g, j):
                t = g * GJ + j
                pe.wait_ge(s_h, t + 1)
                pe.wait_ge(s_hT, t + 2 if j == 0 else t + 1)
                for k in range(KC):
                    last = nc.tensor.transpose(tr_ps[j % 2][:, k * P:(k + 1) * P],
                                               hr[:, j, k * P:(k + 1) * P], ident[:, :])
                last.then_inc(s_tr, 1)

            pe.wait_ge(s_const, 1)
            nc.tensor.matmul(hist_ps[:, 0:NT], zeros_b[:, 0:P], zeros_b[:, 0:NT], start=True, stop=False)
            pe.wait_ge(s_before, 1)
            nc.tensor.matmul(misc_ps[0:NT, 0:1], before[:, :], ones[0:EP, 0:1], start=True,
                             stop=True).then_inc(s_rows, 1)
            pe.wait_ge(s_wA, 16)

            def first_edges():
                pe.wait_ge(s_first, 1)
                nc.tensor.matmul(misc_ps[0:1, 64:64 + NT], row_no[:, 3:4], ident[0:NT, 0:NT], start=True, stop=True)

            def out_of_order():
                pe.wait_ge(s_viol, 1)
                nc.tensor.matmul(misc_ps[0:1, 128:129], viol[:, 0:1], ones[0:EP, 0:1], start=True,
                                 stop=True).then_inc(s_starts, 1)

            def dense_group(g, hist, first=False, hist_last=False):
                transpose_h(g, 0)
                for j in range(GJ):
                    t = g * GJ + j
                    if j + 1 < GJ:
                        transpose_h(g, j + 1)
                    if hist:
                        histogram(t)
                    if hist_last and j == GJ - 1:
                        nc.tensor.matmul(hist_ps[:, 0:NT], zeros_b[:, 0:P], zeros_b[:, 0:NT], start=False,
                                         stop=True).then_inc(s_histend, 1)
                    pe.wait_ge(s_hT, t + 3)
                    pe.wait_ge(s_acc, t + 2 if j == 0 else t + 1)
                    dense(dense_ps[j % 2], hT[j % 2], wA, s_dense)
                    if first and j == 1:
                        first_edges()
                        out_of_order()

            dense_group(0, True, first=True)
            with pe.Fori(1, GA - 1) as g:
                dense_group(g, True)
            dense_group(GA - 1, True, hist_last=True)
            with pe.Fori(GA, NG) as g:
                dense_group(g, False)

            pe.wait_ge(s_flag, 1)
            bad = pe.value_load(flag_i[0:1, 0:1], min_val=0, max_val=1)

            def slots(L, i, u, which):
                n = L * NT + i
                for c in which:
                    hot = hots[:, c * P:(c + 1) * P]
                    pe.wait_ge(s_hot, n * SLOTS + c + 1)
                    if c in SPLIT[L]:
                        b = buffer_of(L, c)
                        pe.wait_ge(s_high, split_no(L, i, c) + 1)
                        nc.tensor.matmul(tx_ps[u][:, :], hot, high[b][:, :], start=c == 0, stop=False)
                        pe.wait_ge(s_low, split_no(L, i, c) + 1)
                        last = nc.tensor.matmul(tx_ps[u][:, :], hot, low[b][:, :], start=False,
                                                stop=c == SLOTS - 1)
                    else:
                        pe.wait_ge(s_gath[c], 16 * (n + 1))
                        last = nc.tensor.matmul(tx_ps[u][:, :], hot.bitcast(F32), rows[:, c, :],
                                                start=c == 0, stop=c == SLOTS - 1)
                    last.then_inc(s_slot, 1)

            zero_row = zeros_b[:, 0:1].to_broadcast([P, D])

            def close(L, i, u):
                n = L * NT + i
                with pe.If(bad > 0):
                    pe.wait_ge(s_greset, n + 1)
                    nc.tensor.matmul(tx_ps[u][:, :], zeros_b[:, :], zero_row, start=True, stop=False)
                    with pe.Fori(0, EC) as e:
                        m = n * EC + e
                        pe.wait_ge(s_ggath, 16 * (e + 1))
                        pe.wait_ge(s_ghot, m + 1)
                        nc.tensor.matmul(tx_ps[u][:, :], gen_hot[:, :], gen_rows, start=False,
                                         stop=False).then_inc(s_gmm, 1)
                    nc.tensor.matmul(tx_ps[u][:, :], zeros_b[:, :], zero_row, start=False, stop=True)
                nc.tensor.matmul(tx_ps[u][:, 0:P], zeros_b[:, 0:P], zeros_b[:, 0:P], start=False, stop=True,
                                 skip_group_check=True).then_inc(s_tx, 1)

            def transpose_tx(L, i):
                pe.wait_ge(s_txs, L * NT + i + 1)
                transposes(tr_ps[0], txs, [s_t1])

            def dense_tx(L, i, w):
                pe.wait_ge(s_txT, L * NT + i + 1)
                pe.wait_ge(s_fin if L else s_mm, i + 1)
                dense(mm_ps, txT, w, s_d1)

            def transpose_h1(i):
                pe.wait_ge(s_h1, i + 1)
                transposes(tr_ps[1], hid, [s_t2])

            def dense_h1(i):
                pe.wait_ge(s_h1T, i + 1)
                pe.wait_ge(s_acc2, i + 1)
                dense(mm2_ps, hidT, wC, s_d2)

            def step(L, i, u):
                slots(L, i, u, range(0, 3))
                transpose_tx(L, i - 1)
                slots(L, i, u, range(3, 6))
                if L == 0:
                    dense_tx(L, i - 1, wB)
                    slots(L, i, u, range(6, 15))
                    transpose_h1(i - 1)
                    slots(L, i, u, range(15, SLOTS))
                    close(L, i, u)
                    dense_h1(i - 1)
                else:
                    dense_tx(L, i - 1, wA)
                    slots(L, i, u, range(6, SLOTS))
                    close(L, i, u)

            pe.wait_ge(s_acc, NT + 2)
            pe.wait_ge(s_wB, 16)
            pe.wait_ge(s_wC, 16)
            for L in range(2):
                if L == 1:
                    pe.wait_ge(s_wD, 16)
                    pe.wait_ge(s_mm, NT + 1)
                slots(L, 0, 0, range(SLOTS))
                close(L, 0, 0)
                with pe.Fori(0, NT // 2 - 1) as k:
                    step(L, 2 * k + 1, 1)
                    step(L, 2 * k + 2, 0)
                step(L, NT - 1, 1)
                transpose_tx(L, NT - 1)
                if L == 0:
                    dense_tx(L, NT - 1, wB)
                    transpose_h1(NT - 1)
                    dense_h1(NT - 1)
                else:
                    dense_tx(L, NT - 1, wA)


_INS = ['x', 'src', 'dst', 'L0_gnn_W1_0', 'L0_gnn_W1_1', 'L0_gnn_b1', 'L0_gnn_gamma', 'L0_gnn_beta',
        'L0_gnn_W2_0', 'L0_gnn_W2_1', 'L0_gnn_b2']


def kernel(**inputs):
    import numpy as _np
    import concourse.bacc as _bacc
    from concourse import mybir as _mybir
    from concourse.bass_utils import run_bass_kernel_spmd as _run

    nc = _bacc.Bacc("TRN2", target_bir_lowering=False, num_devices=1)
    arrays, args = {}, []
    for name in _INS:
        a = _np.ascontiguousarray(inputs[name])
        arrays[f"in_{name}_dram"] = a
        args.append(nc.dram_tensor(f"in_{name}_dram", a.shape, _mybir.dt.from_np(a.dtype), kind="ExternalInput").ap())
    shape = inputs['x'].shape
    args.append(nc.dram_tensor("out_0_dram", shape, _mybir.dt.from_np(_np.dtype("float32")),
                               kind="ExternalOutput").ap())
    gnn_kernel(nc, *args)
    r = _run(nc, [arrays], core_ids=[0])
    return r.results[0]["out_0_dram"]
```

```python
from contextlib import ExitStack

import concourse.bass as bass
from concourse import mybir

F32 = mybir.dt.float32
F32R = mybir.dt.float32r
I32 = mybir.dt.int32
U32 = mybir.dt.uint32
BF16 = mybir.dt.bfloat16
ALU = mybir.AluOpType
ACT = mybir.ActivationFunctionType
AX_X = mybir.AxisListType.X

P = 128
EPS = 1e-5
SLOPE = 0.01


class Count:

    def __init__(self, sem, base=0):
        self.sem, self.base, self.n = sem, base, 0

    def add(self, instruction):
        instruction.then_inc(self.sem, 1)
        self.n += 1

    def settle(self, engine):
        engine.wait_ge(self.sem, self.base + self.n)


def gnn_kernel(nc, x, src, dst, W10, W11, b1, gamma, beta, W20, W21, b2, out):
    N, D = x.shape
    E = src.shape[0]
    KC = D // P
    TR = 125
    NT = N // TR
    TA = 112
    IN = 32
    GJ = 10
    NG = NT // GJ
    SLOTS = 17
    CAP = SLOTS * P
    GW = 8
    SPLIT = (0, 1, 2, 3, 4, 6, 7, 8, 9, 14, 15, 16)
    SR = 4
    assert len(SPLIT) % SR == 0
    EP = 125
    EC = E // EP
    HC = EC // NT
    LAG = 3
    TILE_SHIFT = 22
    TILE_MUL = -(-2**TILE_SHIFT // TR)
    assert NT * TR == N and NT == GJ * NG and EP * EC == E and HC * NT == EC and GJ % 2 == 0 and NT % 2 == 0
    for node in range(N):
        exact = node * TILE_MUL
        for near in (exact * (1 - 2.0**-23), exact * (1 + 2.0**-23)):
            assert int(near) >> TILE_SHIFT == node // TR and near < 2**31

    table = [nc.dram_tensor(f"table{n}", [N, D], F32, kind="Internal").ap() for n in range(2)]

    ctx = ExitStack()
    with ctx:
        def sb(name, shape, dt=F32):
            return ctx.enter_context(nc.sbuf_tensor(name, shape, dt))

        def sem(name):
            return ctx.enter_context(nc.semaphore(name))

        nodes = sb("nodes", [P, NT * D])
        rows = sb("rows", [P, SLOTS, D])
        hots = sb("hots", [P, SLOTS * P], F32R)
        high = [sb(f"high{b}", [P, D], F32R) for b in range(SR)]
        low = [sb(f"low{b}", [P, D], F32R) for b in range(SR)]
        wA = sb("wA", [P, KC, D])
        wB = sb("wB", [P, KC, D])
        bias = sb("bias", [P, D])
        gam = sb("gam", [P, D])
        bet = sb("bet", [P, D])
        ident = sb("ident", [P, P])
        iota_f = sb("iota_f", [P, P])
        part_i = sb("part_i", [P, 1], I32)
        part_f = sb("part_f", [P, 1])
        base_f = sb("base_f", [P, NT])
        idx_all = sb("idx_all", [P, NT * SLOTS], I32)
        loc_all = sb("loc_all", [P, NT * SLOTS], BF16)
        idx_now = sb("idx_now", [P, 2, SLOTS], I32)
        loc_now = sb("loc_now", [P, 2, SLOTS])
        src_i = sb("src_i", [EP, EC], I32)
        dst_f = sb("dst_f", [EP, EC])
        work = sb("work", [P, 6, D])
        sqdeg = sb("sqdeg", [P, NT])
        dinv = sb("dinv", [P, NT])
        ndinv = sb("ndinv", [P, NT])
        ndinv2 = sb("ndinv2", [P, NT])
        ones = sb("ones", [P, 1])
        zeros_b = sb("zeros_b", [P, P], BF16)
        stats = sb("stats", [P, GJ, 6])
        mv = sb("mv", [P, GJ, 2])
        veps = sb("veps", [P, GJ])
        std = sb("std", [P, GJ])
        nxt_i = sb("nxt_i", [EP, 1], I32)
        viol = sb("viol", [EP, 2])
        row_no = sb("row_no", [NT, 4])
        row_i = sb("row_i", [NT, 1], I32)
        flag_f = sb("flag_f", [1, 1])
        flag_i = sb("flag_i", [1, 1], I32)
        gen_idx = sb("gen_idx", [EP, 1], I32)
        gen_loc = sb("gen_loc", [EP, 1])
        gen_hot = sb("gen_hot", [EP, P])

        txs = hid = work[:, 0, :]
        txT = work[:, 1, :]
        xin, stage = work[:, 2, :], work[:, 3, :]
        gen_rows = work[0:EP, 4, :]
        ownT = work[:, 5, :]

        small = work[:, 0:2, :].rearrange("p a b -> p (a b)").rearrange("p (n c) -> p n c", c=64)
        deg1, hasdeg = small[:, 0, 0:NT], small[:, 1, 0:NT]
        before = small[0:EP, 5, 0:NT]
        row_a, row_b = small[0:1, 6, 0:NT], small[0:1, 7, 0:NT]
        first_row = small[0:1, 8, 0:NT + 1]
        flags = small[0:1, 10, 0:1]
        start_i = small[0:1, 9, 0:NT].bitcast(I32)
        iota_i = work[:, 4, 0:P].bitcast(I32)

        xr = rows[:, 0:GJ, :]
        base_i = rows[:, GJ + 6, 0:NT].bitcast(I32)
        rstd_all, nmr_all = rows[:, GJ + 6, NT:2 * NT], rows[:, GJ + 6, 2 * NT:3 * NT]
        scaled = rows[:, 0:GJ, :]
        ids_b = wB[:, 0:2, :].rearrange("p a b -> p (a b)").bitcast(BF16)[0:EP, :]
        r_b, q_b = ids_b[:, 0:EC], ids_b[:, EC:2 * EC]
        picked_i = wB[:, 2:4, :].rearrange("p a b -> p (a b)").bitcast(I32)[0:NT, 0:EC]
        picked = wA[:, 2:4, :].rearrange("p a b -> p (a b)")[0:NT, 0:EC]
        qhot = wA[:, 0:2, :].rearrange("p a b -> p (a b)").bitcast(BF16)[0:EP, 0:2 * NT * HC].rearrange(
            "p (u n c) -> p u n c", u=2, c=HC)
        rhots_view = rows[:, GJ:GJ + 4, :].rearrange("p a b -> p (a b)").bitcast(BF16)
        rhot = rhots_view[0:EP, 0:2 * TR * HC].rearrange("p (u n c) -> p u n c", u=2, c=HC)
        iota_n = rows[:, GJ + 4:GJ + 6, :].rearrange("p a b -> p (a b)").bitcast(BF16)[
            0:EP, 0:TR * HC].rearrange("p (n c) -> p n c", c=HC)
        tmp1 = rows[:, GJ + 2:GJ + 4, :].rearrange("p a b -> p (a b)").bitcast(I32)[0:EP, 0:EC]
        dst_i = rows[:, GJ:GJ + 2, :].rearrange("p a b -> p (a b)").bitcast(I32)[0:EP, 0:EC]
        sortcmp = wA[:, 2:4, :].rearrange("p a b -> p (a b)")[0:EP, 0:EC]
        dst_all = wB[:, 2:4, :].rearrange("p a b -> p (a b)").bitcast(I32)[:, 0:NT * SLOTS]
        dst_all_f = wB[:, 2:4, :].rearrange("p a b -> p (a b)")[:, 0:NT * SLOTS]

        ps = [ctx.enter_context(nc.psum_tensor(f"ps{n}", [P, 512], F32)) for n in range(7)]
        tx_ps, tr_ps, mm_ps, hist_ps, misc_ps = [ps[0], ps[1]], [ps[2], ps[3]], ps[4], ps[5], ps[6]

        s_src, s_dst, s_nxt = sem("src_in"), sem("dst_in"), sem("nxt_in")
        s_wA, s_wB, s_wC, s_wD = sem("w10_in"), sem("w11_in"), sem("w20_in"), sem("w21_in")
        s_b1, s_b2, s_gb = sem("b1_in"), sem("b2_in"), sem("gamma_beta_in")
        s_iota = sem("iota_done")
        s_const = sem("constants_done")
        s_setup = sem("setup_steps")
        s_pad = sem("last_rows_in")
        s_x = [sem(f"x_in{j}") for j in range(GJ)]
        s_aggr = sem("stats_steps")
        s_var, s_std, s_norm = sem("var_ready"), sem("std_ready"), sem("norm_ready")
        s_h = sem("h_ready")
        s_tr = sem("hT_in_psum")
        s_hT = sem("hT_ready")
        s_hhot, s_hist = sem("hist_hots_ready"), sem("hist_hots_used")
        s_histend = sem("hist_ready")
        s_post = sem("post_steps")
        s_deg1, s_sqdeg = sem("deg_ready"), sem("sqrt_deg_ready")
        s_before, s_rows, s_rowno, s_picked = (sem("before_ready"), sem("row_counts_in_psum"),
                                               sem("row_no_ready"), sem("picked_rows_in"))
        s_viol, s_stats = sem("viol_ready"), sem("tile_stats_ready")
        s_first, s_starts = sem("first_ready"), sem("starts_in_psum")
        s_startok = sem("start_index_ready")
        s_flag = sem("flag_ready")
        s_idx = sem("edge_slots_in")
        s_loc = sem("loc_ready")
        s_hs = sem("table_tile_ready")
        s_tab = [sem(f"table0_out{j}") for j in range(GJ)]
        s_gath = [sem(f"slot_rows_in{c}") for c in range(SLOTS)]
        s_pass, s_dpass, s_apass = sem("pool_passed"), sem("vector_passed"), sem("scalar_passed")
        s_idxc = sem("idx_copied")
        s_locc = sem("loc_copied")
        s_hot = sem("hot_ready")
        s_slot = sem("slot_summed")
        s_tx = sem("tx_in_psum")
        s_txs = sem("txs_ready")
        s_t1, s_txT = sem("txT_in_psum"), sem("txT_ready")
        s_ownT = sem("ownT_ready")
        s_d1, s_mm = sem("dense1_in_psum"), sem("dense1_read")
        s_epi = sem("epilogue_steps")
        s_evar, s_estd = sem("epi_var_ready"), sem("epi_std_ready")
        s_high, s_low = sem("high_ready"), sem("low_ready")
        s_h1 = sem("h1_ready")
        s_t2, s_h1T = sem("h1T_in_psum"), sem("h1T_ready")
        s_xb = sem("residual_plus_bias")
        s_xr = sem("residual_in")
        s_hs1 = sem("hs1_ready")
        s_tab1 = sem("table1_out")
        s_fin = sem("out_ready")
        s_out = sem("out_out")
        s_greset = sem("gen_rows_in_reset")
        s_gidx, s_ggath, s_gloc, s_ghot, s_gmm = (sem("gen_idx_copied"), sem("gen_rows_in"),
                                                  sem("gen_loc_ready"), sem("gen_hot_ready"),
                                                  sem("gen_slot_summed"))

        block = ctx.enter_context(nc.Block())

        def node_tile(t):
            return nodes[:, bass.ds(t * D, D)]

        def col(a, t):
            return a[:, bass.ds(t, 1)]

        def split_no(L, i, c):
            return (L * NT + i) * len(SPLIT) + SPLIT.index(c)

        def buffer_of(c):
            return SPLIT.index(c) % SR

        def last_use(L, i, c):
            s = SPLIT.index(c) - SR
            before = SPLIT[s] + (SLOTS if s >= 0 else 0)
            return (L * NT + i) * SLOTS + before + 1

        K_EPI = 5

        def edge_slots(engine, i):
            first = engine.value_load(start_i[0:1, bass.ds(i, 1)], min_val=0, max_val=E - CAP)
            for target, array in ((idx_all, src), (dst_all, dst)):
                engine.dma_start(target[:, bass.ds(i * SLOTS, SLOTS)],
                                 array[bass.ds(first, CAP)].rearrange("(p c) -> p c", p=P)).then_inc(s_idx, 16)

        @block.sync
        def _(sp):
            def rows_of(array, t, n0, n1):
                return array[bass.ds(t * TR + n0, n1 - n0), :]

            def load_tile(target, array, t, s):
                for n0, n1 in ((0, TA), (TA, TR)):
                    sp.dma_start(target[n0:n1, :], rows_of(array, t, n0, n1)).then_inc(s, 16)

            def store_tile(array, t, source, s):
                for n0, n1 in ((0, TA), (TA, TR)):
                    sp.dma_start(rows_of(array, t, n0, n1), source[n0:n1, :]).then_inc(s, 16)

            sp.dma_start(dst_i, dst.rearrange("(p c) -> p c", p=EP)).then_inc(s_dst, 16)
            sp.dma_start(src_i[:, :], src.rearrange("(p c) -> p c", p=EP)).then_inc(s_src, 16)
            sp.dma_start(xr[TR:P, :, :].rearrange("p a b -> p (a b)"),
                         x[0:(P - TR) * GJ, :].rearrange("(p a) n -> p (a n)", p=P - TR)).then_inc(s_pad, 16)
            sp.dma_start(xin[TR:P, :], x[0:P - TR, :]).then_inc(s_pad, 16)
            for j in range(GJ):
                load_tile(xr[:, j, :], x, j, s_x[j])
            sp.dma_start(bias[:, :], b1.partition_broadcast(P)).then_inc(s_b1, 16)
            sp.wait_ge(s_setup, 1)
            with nc.allow_non_contiguous_dma(reason="first edge of each row of the edge list"):
                sp.dma_start(nxt_i[0:EP - 1, :],
                             dst[EC:E].rearrange("(p c) -> p c", c=EC)[:, 0:1]).then_inc(s_nxt, 16)
            sp.dma_start(gam[:, :], gamma.partition_broadcast(P)).then_inc(s_gb, 16)
            sp.dma_start(bet[:, :], beta.partition_broadcast(P)).then_inc(s_gb, 16)

            def next_x(g, j):
                t = g * GJ + j
                sp.wait_ge(s_h, t + 1)
                load_tile(xr[:, j, :], x, t + GJ, s_x[j])

            with sp.Fori(0, NG - 1) as g:
                for j in range(GJ):
                    next_x(g, j)
                sp.wait_ge(s_startok, 1)
                for j in range(0, GJ, 2):
                    edge_slots(sp, g * GJ + j)
            for j in range(0, GJ, 2):
                edge_slots(sp, (NG - 1) * GJ + j)

            with sp.Fori(0, NG) as g:
                for j in range(0, GJ, 2):
                    t = g * GJ + j
                    sp.wait_ge(s_hs, t + 1)
                    store_tile(table[0], t, scaled[:, j, :], s_tab[j])
            sp.dma_start(wA[:, :, :], W10.rearrange("(k p) n -> p k n", p=P)).then_inc(s_wA, 16)
            sp.wait_ge(s_loc, 1)
            sp.dma_start(wB[:, :, :], W11.rearrange("(k p) n -> p k n", p=P)).then_inc(s_wB, 16)

            load_tile(xin, x, 0, s_xr)
            with sp.Fori(0, NT) as i:
                sp.wait_ge(s_hs1, i + 1)
                store_tile(table[1], i, stage, s_tab1)

            sp.wait_ge(s_mm, NT + 1)
            sp.dma_start(wA[:, :, :], W20.rearrange("(k p) n -> p k n", p=P)).then_inc(s_wC, 16)
            sp.dma_start(wB[:, :, :], W21.rearrange("(k p) n -> p k n", p=P)).then_inc(s_wD, 16)
            sp.dma_start(bias[:, :], b2.partition_broadcast(P)).then_inc(s_b2, 16)

            def layer2_io(i, load=True):
                sp.wait_ge(s_fin, i + 2)
                store_tile(out, i, stage, s_out)
                if load:
                    load_tile(xin, x, i + 1, s_xr)

            with sp.Fori(0, NT - 1) as i:
                layer2_io(i)
            layer2_io(NT - 1, load=False)
            sp.wait_ge(s_out, IN * (NT + 1))

        @block.gpsimd
        def _(pool):
            nc.gpsimd.iota(iota_i[:, :], pattern=[[1, P]], base=0, channel_multiplier=0).then_inc(s_iota, 1)
            nc.gpsimd.iota(part_i[:, :], pattern=[[1, 1]], base=0, channel_multiplier=1).then_inc(s_iota, 1)
            nc.gpsimd.iota(base_i[:, :], pattern=[[TR, NT]], base=0, channel_multiplier=0).then_inc(s_iota, 1)

            pool.wait_ge(s_rowno, 1)
            pool.sem_inc(s_pass, 1)
            nc.gpsimd.indirect_dma_start(
                out=picked_i[:, :], out_offset=None, in_=dst.rearrange("(p c) -> p c", p=EP),
                in_offset=bass.IndirectOffsetOnAxis(ap=row_i[:, 0:1].bitcast(U32), axis=0),
            ).then_inc(s_picked, 16)

            with pool.Fori(0, NG) as g:
                for j in range(1, GJ, 2):
                    t = g * GJ + j
                    pool.wait_ge(s_hs, t + 1)
                    pool.sem_inc(s_pass, 1)
                    pool.dma_start(table[0][bass.ds(t * TR, TR), :], scaled[0:TR, j, :]).then_inc(s_tab[j], 16)

            bad = {}

            def gather_tile(L, i, u):
                n = L * NT + i
                pool.wait_ge(s_slot, n * SLOTS + 1)
                pool.wait_ge(s_idxc, n + 1)
                pool.sem_inc(s_pass, 1)
                for c in range(SLOTS):
                    if c % GW == 1:
                        pool.wait_ge(s_slot, n * SLOTS + min(c + GW, SLOTS))
                        pool.sem_inc(s_pass, 1)
                    nc.gpsimd.indirect_dma_start(
                        out=rows[:, c, :], out_offset=None, in_=table[L][:, :],
                        in_offset=bass.IndirectOffsetOnAxis(ap=idx_now[:, u, c:c + 1].bitcast(U32), axis=0),
                    ).then_inc(s_gath[c], 16)
                with pool.If(bad["pool"] > 0):
                    with pool.Fori(0, EC) as e:
                        m = n * EC + e
                        pool.wait_ge(s_gmm, m + 1)
                        nc.gpsimd.tensor_copy(gen_idx[:, :], src_i[:, bass.ds(e, 1)]).then_inc(s_gidx, 1)
                        pool.wait_ge(s_gidx, m + 1)
                        pool.sem_inc(s_pass, 1)
                        nc.gpsimd.indirect_dma_start(
                            out=gen_rows, out_offset=None, in_=table[L][:, :],
                            in_offset=bass.IndirectOffsetOnAxis(ap=gen_idx[:, 0:1].bitcast(U32), axis=0),
                        ).then_inc(s_ggath, 16)
                    pool.wait_ge(s_gmm, (n + 1) * EC + 1)
                    pool.sem_inc(s_pass, 1)
                    nc.gpsimd.inc_swdge_sem([s_ggath], [16 * EC], mode="sub")
                    pool.sem_inc(s_greset, 1)

            pool.wait_ge(s_flag, 1)
            bad["pool"] = pool.value_load(flag_i[0:1, 0:1], min_val=0, max_val=1)
            pool.wait_ge(s_loc, 1)
            for j in range(GJ):
                pool.wait_ge(s_tab[j], (16 if j % 2 else IN) * NG)
            for L in range(2):
                if L == 1:
                    pool.wait_ge(s_tab1, IN * (NT + 1))
                with pool.Fori(0, NT // 2) as k:
                    gather_tile(L, 2 * k, 0)
                    gather_tile(L, 2 * k + 1, 1)

        @block.scalar
        def _(act):
            def take_stds(g):
                act.wait_ge(s_var, g + 1)
                nc.scalar.activation(std[:, :], veps[:, :], ACT.Sqrt).then_inc(s_std, 1)

            def make_h(g, j):
                t = g * GJ + j
                act.wait_ge(s_x[j], IN * (g + 1))
                act.sem_inc(s_apass, 1)
                nc.scalar.activation(node_tile(t), xr[:, j, :], ACT.Relu, bias=col(nmr_all, t),
                                     scale=col(rstd_all, t)).then_inc(s_h, 1)

            with act.Fori(0, NG) as g:
                take_stds(g)
                act.wait_ge(s_norm, g + 1)
                for j in range(GJ):
                    make_h(g, j)
                act.wait_ge(s_startok, 1)
                for j in range(1, GJ, 2):
                    edge_slots(act, g * GJ + j)

            act.wait_ge(s_deg1, 1)
            nc.scalar.activation(sqdeg[:, :], deg1[:, :], ACT.Sqrt).then_inc(s_sqdeg, 1)

            def copy_hT(t, u):
                act.wait_ge(s_tr, t + 1)
                act.sem_inc(s_apass, 1)
                nc.scalar.activation(node_tile(t), tr_ps[u][:, :], ACT.Copy).then_inc(s_hT, 1)

            with act.Fori(0, NT // 2) as k:
                copy_hT(2 * k, 0)
                copy_hT(2 * k + 1, 1)

            def copy_idx(L, i, u):
                if L or not isinstance(i, int):
                    act.wait_ge(s_slot, (L * NT + i) * SLOTS)
                nc.scalar.copy(idx_now[:, u, :], idx_all[:, bass.ds(i * SLOTS, SLOTS)]).then_inc(s_idxc, 1)

            def make_high(L, i, which):
                for c in which:
                    act.wait_ge(s_slot, last_use(L, i, c))
                    act.wait_ge(s_gath[c], 16 * (L * NT + i + 1))
                    nc.scalar.copy(high[buffer_of(c)][:, :], rows[:, c, :]).then_inc(s_high, 1)

            def take_tx(L, i, u):
                n = L * NT + i
                act.wait_ge(s_tx, n + 1)
                act.wait_ge(s_t1, n + 1)
                if L == 0:
                    act.wait_ge(s_t2, i + 1)
                nc.scalar.activation(txs, tx_ps[u][:, :], ACT.Copy,
                                     scale=col(ndinv if L else ndinv2, i)).then_inc(s_txs, 1)

            def copy_txT(L, i):
                n = L * NT + i
                act.wait_ge(s_t1, n + 2)
                act.wait_ge(s_d1, n + 1)
                nc.scalar.copy(txT, tr_ps[0][:, :]).then_inc(s_txT, 1)

            def take_std(i):
                act.wait_ge(s_evar, i + 1)
                nc.scalar.activation(std[:, 0:1], veps[:, 0:1], ACT.Sqrt).then_inc(s_estd, 1)

            def make_hs1(i):
                act.wait_ge(s_h1, i + 1)
                act.wait_ge(s_tab1, IN * (i + 1))
                nc.scalar.activation(stage, hid, ACT.Copy, scale=col(dinv, i)).then_inc(s_hs1, 1)

            def copy_h1T(i):
                act.wait_ge(s_t2, i + 2)
                act.sem_inc(s_apass, 1)
                nc.scalar.activation(node_tile(i), tr_ps[1][:, :], ACT.Copy).then_inc(s_h1T, 1)

            def copy_own(L, i):
                if L or not isinstance(i, int):
                    act.wait_ge(s_d1, L * NT + i)
                act.sem_inc(s_apass, 1)
                nc.scalar.activation(ownT, node_tile(i), ACT.Copy).then_inc(s_ownT, 1)

            def act_step(L, i, u, prev=True, more=True):
                def highs(first, end):
                    make_high(L, i, [c for c in SPLIT if first <= c < end])

                highs(0, 3)
                if prev:
                    take_tx(L, i - 1, 1 - u)
                highs(3, 4)
                if more:
                    copy_idx(L, i + 1, 1 - u)
                highs(4, 7)
                copy_own(L, i)
                if prev:
                    copy_txT(L, i - 1)
                highs(7, 10)
                if prev and L == 0:
                    take_std(i - 1)
                highs(10, 16)
                if prev and L == 0:
                    make_hs1(i - 1)
                highs(16, SLOTS)
                if prev and L == 0:
                    copy_h1T(i - 1)

            act.wait_ge(s_loc, 1)
            for L in range(2):
                copy_idx(L, 0, 0)
                if L == 1:
                    act.wait_ge(s_t2, NT + 1)
                act_step(L, 0, 0, prev=False)
                with act.Fori(0, NT // 2 - 1) as k:
                    act_step(L, 2 * k + 1, 1)
                    act_step(L, 2 * k + 2, 0)
                act_step(L, NT - 1, 1, more=False)
                take_tx(L, NT - 1, 1)
                copy_txT(L, NT - 1)
                if L == 0:
                    take_std(NT - 1)
                    make_hs1(NT - 1)
                    copy_h1T(NT - 1)

        @block.vector
        def _(dve):
            own = Count(s_setup)
            dve.sem_inc(s_hT, 2)
            dve.sem_inc(s_hist, 2)
            dve.sem_inc(s_slot, SLOTS)
            dve.sem_inc(s_t1, 1)
            dve.sem_inc(s_d1, 1)
            dve.sem_inc(s_t2, 1)
            dve.sem_inc(s_fin, 1)
            dve.sem_inc(s_mm, 1)
            dve.sem_inc(s_gmm, 1)
            dve.sem_inc(s_greset, 1)
            dve.sem_inc(s_tab1, IN)
            dve.sem_inc(s_out, IN)
            own.add(nc.vector.memset(nxt_i[:, :], N))
            own.add(nc.vector.memset(ones[:, :], 1.0))
            own.add(nc.vector.memset(zeros_b[:, :], 0.0))
            dve.wait_ge(s_iota, 3)
            own.add(nc.vector.tensor_copy(iota_f[:, :], iota_i[:, :]))
            own.add(nc.vector.tensor_copy(part_f[:, :], part_i[:, :]))
            own.add(nc.vector.tensor_copy(base_f[:, :], base_i[:, :]))
            own.settle(dve)
            own.add(nc.vector.tensor_scalar(ident[:, :], iota_f[:, :], part_f[:, 0:1], None, ALU.is_equal))
            own.settle(dve)
            nc.vector.tensor_copy(flag_f[:, :], ones[0:1, 0:1]).then_inc(s_const, 1)

            def search_rows():
                dve.wait_ge(s_dst, 16)
                own.add(nc.vector.tensor_copy(dst_f[:, :], dst_i))
                own.settle(dve)
                nc.vector.tensor_scalar(before[:, :], base_f[0:EP, :], dst_f[:, 0:1], None,
                                        ALU.is_gt).then_inc(s_before, 1)
                dve.wait_ge(s_rows, 1)
                own.add(nc.vector.tensor_scalar(row_no[:, 0:1], misc_ps[0:NT, 0:1], -1.0, 0.0, ALU.add, ALU.max))
                own.settle(dve)
                nc.vector.tensor_copy(row_i[:, :], row_no[:, 0:1]).then_inc(s_rowno, 1)

            def edge_ids():
                dve.wait_ge(s_src, 16)
                own.add(nc.vector.tensor_scalar(tmp1, src_i[:, :], float(TILE_MUL), None, ALU.mult))
                own.settle(dve)
                own.add(nc.vector.tensor_single_scalar(tmp1, tmp1, TILE_SHIFT, ALU.logical_shift_right))
                own.settle(dve)
                own.add(nc.vector.tensor_copy(q_b, tmp1))
                own.add(nc.vector.scalar_tensor_tensor(out=r_b, in0=tmp1, scalar=-float(TR), in1=src_i[:, :],
                                                       op0=ALU.mult, op1=ALU.add))
                own.add(nc.vector.tensor_copy(iota_n, iota_f[0:EP, 0:TR].unsqueeze(2).to_broadcast([EP, TR, HC])))
                own.settle(dve)

            def order():
                dve.wait_ge(s_nxt, 16)
                own.add(nc.vector.tensor_copy(viol[:, 1:2], nxt_i[:, :]))
                own.add(nc.vector.tensor_tensor(sortcmp[:, 0:EC - 1], dst_f[:, 0:EC - 1], dst_f[:, 1:EC], ALU.is_gt))
                own.settle(dve)
                own.add(nc.vector.tensor_tensor(sortcmp[:, EC - 1:EC], dst_f[:, EC - 1:EC], viol[:, 1:2], ALU.is_gt))
                own.settle(dve)
                nc.vector.reduce_max(viol[:, 0:1], sortcmp, AX_X).then_inc(s_viol, 1)

            def search_within():
                dve.wait_ge(s_picked, 16)
                own.add(nc.vector.tensor_copy(picked[:, :], picked_i[:, :]))
                own.add(nc.vector.tensor_scalar(row_no[:, 1:2], part_f[0:NT, :], float(TR), None, ALU.mult))
                own.settle(dve)
                own.add(nc.vector.tensor_scalar(picked[:, :], picked[:, :], row_no[:, 1:2], None, ALU.is_lt))
                own.settle(dve)
                own.add(nc.vector.reduce_sum(row_no[:, 2:3], picked[:, :], AX_X))
                own.settle(dve)
                nc.vector.scalar_tensor_tensor(out=row_no[:, 3:4], in0=row_no[:, 0:1], scalar=float(EC),
                                               in1=row_no[:, 2:3], op0=ALU.mult, op1=ALU.add).then_inc(s_first, 1)

            def start_rows():
                dve.wait_ge(s_starts, 1)
                own.add(nc.vector.tensor_copy(first_row[:, 0:NT], misc_ps[0:1, 64:64 + NT]))
                own.add(nc.vector.memset(first_row[:, NT:NT + 1], float(E)))
                own.add(nc.vector.tensor_copy(flag_f[:, :], misc_ps[0:1, 128:129]))
                own.settle(dve)
                own.add(nc.vector.tensor_scalar_min(row_a[:, :], first_row[:, 0:NT], float(E - CAP)))
                own.settle(dve)
                nc.vector.tensor_copy(start_i[:, :], row_a[:, :]).then_inc(s_startok, 1)
                own.add(nc.vector.tensor_tensor(row_b[:, :], first_row[:, 1:NT + 1], row_a[:, :], ALU.subtract))
                own.settle(dve)
                own.add(nc.vector.tensor_scalar(row_b[:, :], row_b[:, :], float(CAP), None, ALU.is_gt))
                own.settle(dve)
                own.add(nc.vector.reduce_max(flags[:, :], row_b[:, :], AX_X))
                own.settle(dve)
                own.add(nc.vector.tensor_tensor(flag_f[:, :], flag_f[:, :], flags[:, :], ALU.max))
                own.settle(dve)
                own.add(nc.vector.tensor_scalar(flag_f[:, :], flag_f[:, :], 0.0, None, ALU.is_gt))
                own.settle(dve)
                nc.vector.tensor_copy(flag_i[:, :], flag_f[:, :]).then_inc(s_flag, 1)

            def hist_hots(t, u):
                columns = bass.ds(t * HC, HC)
                dve.wait_ge(s_hist, t + 1)
                nc.vector.tensor_tensor(rhot[:, u], iota_n, r_b[:, columns].unsqueeze(1).to_broadcast([EP, TR, HC]),
                                        ALU.is_equal).then_inc(s_hhot, 1)
                nc.vector.tensor_tensor(qhot[:, u], iota_n[:, 0:NT, :],
                                        q_b[:, columns].unsqueeze(1).to_broadcast([EP, NT, HC]),
                                        ALU.is_equal).then_inc(s_hhot, 1)

            def stats_of(g, j):
                dve.wait_ge(s_x[j], IN * (g + 1))
                nc.vector.bn_stats(stats[:, j, :], xr[:, j, :]).then_inc(s_stats, 1)

            def group_var(g):
                dve.wait_ge(s_stats, GJ * (g + 1))
                dve.sem_inc(s_dpass, 1)
                for j in range(GJ):
                    last = nc.vector.bn_aggr(mv[:, j, :], stats[:, j, :])
                last.then_inc(s_aggr, 1)
                dve.wait_ge(s_aggr, 2 * g + 1)
                nc.vector.tensor_scalar_add(veps[:, :], mv[:, :, 1], EPS).then_inc(s_var, 1)

            def group_norm(g):
                dve.wait_ge(s_std, g + 1)
                nc.vector.reciprocal(rstd_all[:, bass.ds(g * GJ, GJ)], std[:, :]).then_inc(s_aggr, 1)
                dve.wait_ge(s_aggr, 2 * g + 2)
                nc.vector.scalar_tensor_tensor(out=nmr_all[:, bass.ds(g * GJ, GJ)], in0=mv[:, :, 0], scalar=-1.0,
                                               in1=rstd_all[:, bass.ds(g * GJ, GJ)], op0=ALU.mult,
                                               op1=ALU.mult).then_inc(s_norm, 1)

            def hist_group(g, first=False, more=True):
                for j in range(GJ):
                    hist_hots(g * GJ + j, j % 2)
                    if j == 0:
                        group_norm(g)
                    if first and j == 1:
                        search_within()
                    if first and j == 2:
                        order()
                    if first and j == 3:
                        start_rows()
                    if more and j >= LAG:
                        stats_of(g + 1, j - LAG)
                if more:
                    for j in range(GJ - LAG, GJ):
                        stats_of(g + 1, j)
                    group_var(g + 1)

            search_rows()
            edge_ids()
            dve.wait_ge(s_pad, 32)
            for j in range(GJ):
                stats_of(0, j)
            group_var(0)
            hist_group(0, first=True)
            with dve.Fori(1, NG - 1) as g:
                hist_group(g)
            hist_group(NG - 1, more=False)

            post = Count(s_post)
            dve.wait_ge(s_histend, 1)
            nc.vector.tensor_scalar_max(deg1[:, :], hist_ps[:, 0:NT], 1.0).then_inc(s_deg1, 1)
            post.add(nc.vector.tensor_scalar(hasdeg[:, :], hist_ps[:, 0:NT], 0.0, None, ALU.is_gt))
            dve.wait_ge(s_sqdeg, 1)
            post.add(nc.vector.reciprocal(dinv[:, :], sqdeg[:, :]))
            post.settle(dve)
            post.add(nc.vector.scalar_tensor_tensor(out=ndinv[:, :], in0=dinv[:, :], scalar=-1.0,
                                                    in1=hasdeg[:, :], op0=ALU.mult, op1=ALU.mult))
            post.settle(dve)
            post.add(nc.vector.tensor_tensor(ndinv2[:, :], ndinv[:, :], dinv[:, :], ALU.mult))
            post.settle(dve)

            dve.wait_ge(s_h, NT)

            def table_group(g, first=False):
                for j in range(GJ):
                    t = g * GJ + j
                    if not first:
                        dve.wait_ge(s_tr, t - GJ + 1)
                        dve.wait_ge(s_tab[j], (16 if j % 2 else IN) * g)
                    nc.vector.tensor_scalar(scaled[:, j, :], node_tile(t), col(dinv, t), None,
                                            ALU.mult).then_inc(s_hs, 1)

            table_group(0, first=True)
            with dve.Fori(1, NG) as g:
                table_group(g)

            dve.wait_ge(s_idx, 2 * 16 * NT)
            post.add(nc.vector.tensor_copy(dst_all_f, dst_all))
            post.settle(dve)
            nc.vector.tensor_tensor(loc_all[:, :].rearrange("p (i c) -> p i c", c=SLOTS),
                                    dst_all_f.rearrange("p (i c) -> p i c", c=SLOTS),
                                    base_f[:, :].unsqueeze(2).to_broadcast([P, NT, SLOTS]),
                                    ALU.subtract).then_inc(s_loc, 1)
            dve.wait_ge(s_loc, 1)
            dve.wait_ge(s_flag, 1)
            bad = dve.value_load(flag_i[0:1, 0:1], min_val=0, max_val=1)

            def copy_loc(L, i, u):
                dve.wait_ge(s_slot, (L * NT + i) * SLOTS + 1)
                nc.vector.tensor_copy(loc_now[:, u, :], loc_all[:, bass.ds(i * SLOTS, SLOTS)]).then_inc(s_locc, 1)
                dve.wait_ge(s_locc, L * NT + i + 1)

            def hots_of(L, i, u, first, end):
                n = L * NT + i
                for c in range(first, end):
                    dve.wait_ge(s_slot, n * SLOTS + c + 1)
                    nc.vector.tensor_scalar(hots[:, c * P:(c + 1) * P], iota_f[:, :], loc_now[:, u, c:c + 1],
                                            None, ALU.is_equal).then_inc(s_hot, 1)

            def make_low(L, i, c):
                b = buffer_of(c)
                dve.wait_ge(s_high, split_no(L, i, c) + 1)
                nc.vector.tensor_tensor(low[b][:, :], rows[:, c, :], high[b][:, :].bitcast(F32),
                                        ALU.subtract).then_inc(s_low, 1)

            def general(L, i):
                n = L * NT + i
                with dve.If(bad > 0):
                    with dve.Fori(0, EC) as e:
                        m = n * EC + e
                        dve.wait_ge(s_gmm, m + 1)
                        nc.vector.tensor_tensor(gen_loc[:, :], dst_f[:, bass.ds(e, 1)],
                                                base_f[0:EP, bass.ds(i, 1)], ALU.subtract).then_inc(s_gloc, 1)
                        dve.wait_ge(s_gloc, m + 1)
                        nc.vector.tensor_scalar(gen_hot[:, :], iota_f[0:EP, :], gen_loc[:, 0:1], None,
                                                ALU.is_equal).then_inc(s_ghot, 1)

            def conv_stats(i):
                own = Count(s_epi, i * K_EPI)
                dve.wait_ge(s_d1, i + 2)
                nc.vector.scalar_tensor_tensor(out=hid, in0=mm_ps[:, :], scalar=col(sqdeg, i), in1=bias[:, :],
                                               op0=ALU.mult, op1=ALU.add).then_inc(s_mm, 1)
                dve.wait_ge(s_mm, i + 2)
                own.add(nc.vector.bn_stats(stats[:, 0, :], hid))
                own.settle(dve)
                dve.sem_inc(s_dpass, 1)
                own.add(nc.vector.bn_aggr(mv[:, 0, :], stats[:, 0, :]))
                own.settle(dve)
                nc.vector.tensor_scalar_add(veps[:, 0:1], mv[:, 0, 1:2], EPS).then_inc(s_evar, 1)
                own.add(nc.vector.scalar_tensor_tensor(out=hid, in0=hid, scalar=mv[:, 0, 0:1], in1=gam[:, :],
                                                       op0=ALU.subtract, op1=ALU.mult))
                return own

            def norm1(i, own):
                dve.wait_ge(s_estd, i + 1)
                own.add(nc.vector.reciprocal(veps[:, 1:2], std[:, 0:1]))
                own.settle(dve)
                own.add(nc.vector.scalar_tensor_tensor(out=hid, in0=hid, scalar=veps[:, 1:2], in1=bet[:, :],
                                                       op0=ALU.mult, op1=ALU.add))
                own.settle(dve)
                nc.vector.scalar_tensor_tensor(out=hid, in0=hid, scalar=SLOPE, in1=hid, op0=ALU.mult,
                                               op1=ALU.max).then_inc(s_h1, 1)
                assert own.n == K_EPI

            def finish2(i):
                dve.wait_ge(s_xr, IN * (i + 1))
                nc.vector.tensor_tensor(xin, xin, bias[:, :], ALU.add).then_inc(s_xb, 1)
                dve.wait_ge(s_xb, i + 1)
                dve.wait_ge(s_d1, NT + i + 2)
                dve.wait_ge(s_out, IN * (i + 1))
                nc.vector.tensor_tensor(stage, mm_ps[:, :], xin, ALU.add).then_inc(s_fin, 1)

            LATE = 14

            def dve_step(L, i, u, prev=True, more=True):
                def low(*which):
                    for c in which:
                        make_low(L, i, c)

                def next_hots(first, end):
                    if more:
                        if first == 0:
                            copy_loc(L, i + 1, 1 - u)
                        hots_of(L, i + 1, 1 - u, first, end)

                low(0, 1)
                if prev:
                    hots_of(L, i, u, LATE, SLOTS)
                low(2, 3)
                next_hots(0, 1)
                low(4)
                next_hots(1, 2)
                low(6, 7)
                next_hots(2, 4)
                low(8, 9)
                next_hots(4, 6)
                if prev and L == 0:
                    own = conv_stats(i - 1)
                    norm1(i - 1, own)
                elif prev:
                    finish2(i - 1)
                low(14, 15, 16)
                next_hots(6, LATE)
                general(L, i)

            dve.wait_ge(s_gb, 32)
            dve.wait_ge(s_b1, 16)
            for L in range(2):
                if L == 1:
                    dve.wait_ge(s_tab1, IN * (NT + 1))
                    dve.wait_ge(s_b2, 16)
                copy_loc(L, 0, 0)
                hots_of(L, 0, 0, 0, SLOTS)
                dve_step(L, 0, 0, prev=False)
                with dve.Fori(0, NT // 2 - 1) as k:
                    dve_step(L, 2 * k + 1, 1)
                    dve_step(L, 2 * k + 2, 0)
                dve_step(L, NT - 1, 1, more=False)
                if L == 0:
                    own = conv_stats(NT - 1)
                    norm1(NT - 1, own)
                else:
                    finish2(NT - 1)

        @block.tensor
        def _(pe):
            def transposes(to, source, signal):
                for k in range(KC):
                    last = nc.tensor.transpose(to[:, k * P:(k + 1) * P], source[:, k * P:(k + 1) * P], ident[:, :])
                for s in signal:
                    last.then_inc(s, 1)

            def dense(to, source, w, start, stop):
                for k in range(KC):
                    last = nc.tensor.matmul(to[:, :], source[:, k * P:(k + 1) * P], w[:, k, :],
                                            start=start and k == 0, stop=stop and k == KC - 1)
                return last

            def histogram(t, u):
                pe.wait_ge(s_hhot, 2 * t + 2)
                for c in range(HC):
                    last = nc.tensor.matmul(hist_ps[0:TR, 0:NT], rhot[:, u, :, c], qhot[:, u, :, c],
                                            start=False, stop=False)
                last.then_inc(s_hist, 1)

            pe.wait_ge(s_const, 1)
            nc.tensor.matmul(hist_ps[:, 0:NT], zeros_b[:, 0:P], zeros_b[:, 0:NT], start=True, stop=False)
            pe.wait_ge(s_before, 1)
            nc.tensor.matmul(misc_ps[0:NT, 0:1], before[:, :], ones[0:EP, 0:1], start=True,
                             stop=True).then_inc(s_rows, 1)
            histogram(0, 0)
            histogram(1, 1)
            pe.wait_ge(s_first, 1)
            nc.tensor.matmul(misc_ps[0:1, 64:64 + NT], row_no[:, 3:4], ident[0:NT, 0:NT], start=True, stop=True)
            histogram(2, 0)
            pe.wait_ge(s_viol, 1)
            nc.tensor.matmul(misc_ps[0:1, 128:129], viol[:, 0:1], ones[0:EP, 0:1], start=True,
                             stop=True).then_inc(s_starts, 1)
            histogram(3, 1)
            with pe.Fori(2, NT // 2) as k:
                histogram(2 * k, 0)
                histogram(2 * k + 1, 1)
            nc.tensor.matmul(hist_ps[:, 0:NT], zeros_b[:, 0:P], zeros_b[:, 0:NT], start=False,
                             stop=True).then_inc(s_histend, 1)

            def transpose_h(g, j):
                t = g * GJ + j
                pe.wait_ge(s_hs, t + 1)
                pe.wait_ge(s_hT, t + 1)
                transposes(tr_ps[j % 2], scaled[:, j, :], [s_tr])

            with pe.Fori(0, NG) as g:
                for j in range(GJ):
                    transpose_h(g, j)

            pe.wait_ge(s_flag, 1)
            bad = pe.value_load(flag_i[0:1, 0:1], min_val=0, max_val=1)

            def slots(L, i, u, which):
                n = L * NT + i
                for c in which:
                    hot = hots[:, c * P:(c + 1) * P]
                    pe.wait_ge(s_hot, n * SLOTS + c + 1)
                    if c in SPLIT:
                        b = buffer_of(c)
                        pe.wait_ge(s_high, split_no(L, i, c) + 1)
                        nc.tensor.matmul(tx_ps[u][:, :], hot, high[b][:, :], start=c == 0, stop=False)
                        pe.wait_ge(s_low, split_no(L, i, c) + 1)
                        last = nc.tensor.matmul(tx_ps[u][:, :], hot, low[b][:, :], start=False,
                                                stop=c == SLOTS - 1)
                    else:
                        pe.wait_ge(s_gath[c], 16 * (n + 1))
                        last = nc.tensor.matmul(tx_ps[u][:, :], hot.bitcast(F32), rows[:, c, :],
                                                start=c == 0, stop=c == SLOTS - 1)
                    last.then_inc(s_slot, 1)

            zero_row = zeros_b[:, 0:1].to_broadcast([P, D])

            def close(L, i, u):
                n = L * NT + i
                with pe.If(bad > 0):
                    pe.wait_ge(s_greset, n + 1)
                    nc.tensor.matmul(tx_ps[u][:, :], zeros_b[:, :], zero_row, start=True, stop=False)
                    with pe.Fori(0, EC) as e:
                        m = n * EC + e
                        pe.wait_ge(s_ggath, 16 * (e + 1))
                        pe.wait_ge(s_ghot, m + 1)
                        nc.tensor.matmul(tx_ps[u][:, :], gen_hot[:, :], gen_rows, start=False,
                                         stop=False).then_inc(s_gmm, 1)
                    nc.tensor.matmul(tx_ps[u][:, :], zeros_b[:, :], zero_row, start=False, stop=True)
                nc.tensor.matmul(tx_ps[u][:, 0:P], zeros_b[:, 0:P], zeros_b[:, 0:P], start=False, stop=True,
                                 skip_group_check=True).then_inc(s_tx, 1)

            def transpose_tx(L, i):
                pe.wait_ge(s_txs, L * NT + i + 1)
                transposes(tr_ps[0], txs, [s_t1])

            def dense_own(L, i):
                pe.wait_ge(s_fin if L else s_mm, i + 1)
                pe.wait_ge(s_ownT, L * NT + i + 1)
                dense(mm_ps, ownT, wA, True, False)

            def dense_tx(L, i):
                pe.wait_ge(s_txT, L * NT + i + 1)
                dense(mm_ps, txT, wB, False, True).then_inc(s_d1, 1)

            def transpose_h1(i):
                pe.wait_ge(s_h1, i + 1)
                transposes(tr_ps[1], hid, [s_t2])

            def step(L, i, u, prev=True):
                slots(L, i, u, range(0, 3))
                if prev:
                    transpose_tx(L, i - 1)
                slots(L, i, u, range(3, 6))
                if prev:
                    dense_tx(L, i - 1)
                slots(L, i, u, range(6, 15))
                if prev and L == 0:
                    transpose_h1(i - 1)
                slots(L, i, u, range(15, SLOTS))
                close(L, i, u)
                dense_own(L, i)

            pe.wait_ge(s_hT, NT + 2)
            for L in range(2):
                if L == 0:
                    pe.wait_ge(s_wA, 16)
                    pe.wait_ge(s_wB, 16)
                else:
                    pe.wait_ge(s_wC, 16)
                    pe.wait_ge(s_wD, 16)
                    pe.wait_ge(s_h1T, NT)
                    pe.wait_ge(s_mm, NT + 1)
                step(L, 0, 0, prev=False)
                with pe.Fori(0, NT // 2 - 1) as k:
                    step(L, 2 * k + 1, 1)
                    step(L, 2 * k + 2, 0)
                step(L, NT - 1, 1)
                transpose_tx(L, NT - 1)
                dense_tx(L, NT - 1)
                if L == 0:
                    transpose_h1(NT - 1)


_INS = ['x', 'src', 'dst', 'L0_gnn_W1_0', 'L0_gnn_W1_1', 'L0_gnn_b1', 'L0_gnn_gamma', 'L0_gnn_beta',
        'L0_gnn_W2_0', 'L0_gnn_W2_1', 'L0_gnn_b2']


def kernel(**inputs):
    import numpy as _np
    import concourse.bacc as _bacc
    from concourse import mybir as _mybir
    from concourse.bass_utils import run_bass_kernel_spmd as _run

    nc = _bacc.Bacc("TRN2", target_bir_lowering=False, num_devices=1)
    arrays, args = {}, []
    for name in _INS:
        a = _np.ascontiguousarray(inputs[name])
        arrays[f"in_{name}_dram"] = a
        args.append(nc.dram_tensor(f"in_{name}_dram", a.shape, _mybir.dt.from_np(a.dtype), kind="ExternalInput").ap())
    shape = inputs['x'].shape
    args.append(nc.dram_tensor("out_0_dram", shape, _mybir.dt.from_np(_np.dtype("float32")),
                               kind="ExternalOutput").ap())
    gnn_kernel(nc, *args)
    r = _run(nc, [arrays], core_ids=[0])
    return r.results[0]["out_0_dram"]
```
